# Optimizing a Trainium2 kernel written in Bass

```python
import numpy as np
import jax
import jax.numpy as jnp

def _softmax(x, axis=-1):
    return jax.nn.softmax(x, axis=axis)

def _gelu(x):
    return jax.nn.gelu(x, approximate=True)

def _silu(x):
    return jax.nn.silu(x)

def _sigmoid(x):
    return jax.nn.sigmoid(x)

def _layernorm(x, axis=-1, eps=1e-05):
    m = jnp.mean(x, axis=axis, keepdims=True)
    v = jnp.var(x, axis=axis, keepdims=True)
    return (x - m) / jnp.sqrt(v + eps)

def _scatter_add(tgt, idx, src, axis=0):
    return tgt.at[idx].add(src)

def _segment_sum(src, seg, n):
    return jax.ops.segment_sum(src, seg, n)
kernel_name = 'mk_early_fusion_d2_tok_img256_r4_4976a1'

def setup_inputs(seed: int=0):
    np.random.seed(seed)
    _w = jnp.asarray

    def _rec_inputs():
        import jax
        import jax.numpy as jnp
        _rk = jax.random.key(seed)
        x = -7.10856e-05 + 0.999911 * jax.random.normal(jax.random.fold_in(_rk, 1), (4, 64, 128, 64), jnp.float32)
        txt = -0.000161634 + 0.479995 * jax.random.normal(jax.random.fold_in(_rk, 2), (4, 77, 64), jnp.float32)
        return (x, txt)
    x, txt = _rec_inputs()

    def _L0_tok_setup():
        import jax, jax.numpy as jnp
        import numpy as np
        PATCH_LEN = 16
        STRIDE = 8
        PAD = 8
        key = jax.random.key(seed)
        k1, k2 = jax.random.split(key)
        x = jax.random.normal(k1, (32, 64, 128, 64), dtype=jnp.float32)
        in_feat = 64 * (PATCH_LEN // 2 + 1) * 2
        W = jax.random.normal(k2, (64, in_feat), dtype=jnp.float32) * 0.02
        return {'x': x, 'W': W}
    _L0_tok_all = _L0_tok_setup()
    _L0_tok_in = {k: v for k, v in _L0_tok_all.items() if k in ('W',)}
    del _L0_tok_all

    def _L0_attn_setup():
        import jax, jax.numpy as jnp
        import numpy as np
        B, T, H, D, N, R, K = (2, 256, 64, 256, 16, 16, 4)
        EPS = 1e-05

        def layer_norm(x, g, b):
            m = jnp.mean(x, -1, keepdims=True)
            v = jnp.mean((x - m) ** 2, -1, keepdims=True)
            return (x - m) * jax.lax.rsqrt(v + EPS) * g + b

        def rms_norm(x, w):
            return x * jax.lax.rsqrt(jnp.mean(x * x, -1, keepdims=True) + EPS) * w

        def selective_scan(u, dt, A, Bm, Cm, Dp):
            dA = jnp.exp(dt[..., None] * A)
            dBu = (dt * u)[..., None] * Bm[:, :, None, :]

            def step(h, inp):
                dA_t, dBu_t, C_t = inp
                h = dA_t * h + dBu_t
                return (h, jnp.einsum('bdn,bn->bd', h, C_t))
            h0 = jnp.zeros((u.shape[0], u.shape[2], A.shape[1]), u.dtype)
            _, ys = jax.lax.scan(step, h0, (dA.swapaxes(0, 1), dBu.swapaxes(0, 1), Cm.swapaxes(0, 1)))
            return ys.swapaxes(0, 1) + u * Dp

        def mamba_mixer(h, inproj_w, conv_w, conv_b, xproj_w, dtproj_w, dtproj_b, A_log, Dp, outproj_w):
            proj = jnp.einsum('bth,eh->bte', h, inproj_w)
            u, gate = (proj[..., :D], proj[..., D:])
            uc = jax.lax.conv_general_dilated(u.swapaxes(1, 2), conv_w, (1,), [(K - 1, 0)], dimension_numbers=('NCH', 'OIH', 'NCH'), feature_group_count=D)
            u = jax.nn.silu(uc + conv_b[None, :, None]).swapaxes(1, 2)
            ssm = jnp.einsum('btd,ed->bte', u, xproj_w)
            dt_r, Bm, Cm = (ssm[..., :R], ssm[..., R:R + N], ssm[..., R + N:])
            dt = jax.nn.softplus(jnp.einsum('btr,dr->btd', dt_r, dtproj_w) + dtproj_b)
            A = -jnp.exp(A_log)
            y = selective_scan(u, dt, A, Bm, Cm, Dp)
            y = y * jax.nn.silu(gate)
            return jnp.einsum('btd,hd->bth', y, outproj_w)

        def _forward(x, pre_g, pre_b, post_g, post_b, norm_w, inproj_w, conv_w, conv_b, xproj_w, dtproj_w, dtproj_b, A_log, D_param, outproj_w, normf_w):
            h = layer_norm(x, pre_g, pre_b)
            for i in range(2):
                h = h + mamba_mixer(rms_norm(h, norm_w[i]), inproj_w[i], conv_w[i], conv_b[i], xproj_w[i], dtproj_w[i], dtproj_b[i], A_log[i], D_param[i], outproj_w[i])
            h = rms_norm(h, normf_w)
            return layer_norm(h, post_g, post_b)
        key = jax.random.key(seed)
        ks = jax.random.split(key, 8)
        s = 0.05
        A0 = jnp.log(jnp.arange(1, N + 1, dtype=jnp.float32))
        return {'x': jax.random.normal(ks[0], (B, T, H), jnp.float32), 'pre_g': jnp.ones((H,), jnp.float32), 'pre_b': jnp.zeros((H,), jnp.float32), 'post_g': jnp.ones((H,), jnp.float32), 'post_b': jnp.zeros((H,), jnp.float32), 'norm_w': jnp.ones((2, H), jnp.float32), 'inproj_w': jax.random.normal(ks[1], (2, 2 * D, H), jnp.float32) * s, 'conv_w': jax.random.normal(ks[2], (2, D, 1, K), jnp.float32) * s, 'conv_b': jnp.zeros((2, D), jnp.float32), 'xproj_w': jax.random.normal(ks[3], (2, R + 2 * N, D), jnp.float32) * s, 'dtproj_w': jax.random.normal(ks[4], (2, D, R), jnp.float32) * s, 'dtproj_b': jax.random.normal(ks[5], (2, D), jnp.float32) * s, 'A_log': jnp.broadcast_to(A0, (2, D, N)) + 0.0, 'D_param': jnp.ones((2, D), jnp.float32), 'outproj_w': jax.random.normal(ks[6], (2, H, D), jnp.float32) * s, 'normf_w': jnp.ones((H,), jnp.float32)}
    _L0_attn_all = _L0_attn_setup()
    _L0_attn_in = {k: v for k, v in _L0_attn_all.items() if k in ('pre_g', 'pre_b', 'post_g', 'post_b', 'norm_w', 'inproj_w', 'conv_w', 'conv_b', 'xproj_w', 'dtproj_w', 'dtproj_b', 'A_log', 'D_param', 'outproj_w', 'normf_w')}
    del _L0_attn_all

    def _L0_ffn_setup():
        import jax, jax.numpy as jnp
        import numpy as np
        E = 8
        K = 2
        D = 64
        H = 128
        DOUT = 64
        EPS = 1e-05
        key = jax.random.key(seed)
        ks = jax.random.split(key, 9)
        s = 0.02
        return {'x': jax.random.normal(ks[0], (4, 2048, D), jnp.float32), 'gamma': 1.0 + 0.05 * jax.random.normal(ks[1], (D,), jnp.float32), 'beta': 0.05 * jax.random.normal(ks[2], (D,), jnp.float32), 'Wr': 0.01 * jax.random.normal(ks[3], (D, E), jnp.float32), 'br': jnp.zeros((E,), jnp.float32), 'W1': s * jax.random.normal(ks[4], (E, D, H), jnp.float32), 'b1': s * jax.random.normal(ks[5], (E, H), jnp.float32), 'W2': s * jax.random.normal(ks[6], (E, H, DOUT), jnp.float32), 'b2': s * jax.random.normal(ks[7], (E, DOUT), jnp.float32)}
    _L0_ffn_all = _L0_ffn_setup()
    _L0_ffn_in = {k: v for k, v in _L0_ffn_all.items() if k in ('gamma', 'beta', 'Wr', 'br', 'W1', 'b1', 'W2', 'b2')}
    del _L0_ffn_all

    def _L1_attn_setup():
        import jax, jax.numpy as jnp
        import numpy as np
        K = 24

        def _lds(xs, A, Bv, C, M):
            N, L = xs.shape
            S = A.shape[0]

            def step(h, xt):
                h = h * A[None, :] + xt[:, None] * Bv[None, :]
                return (h, h @ C)
            h0 = jnp.zeros((N, S), xs.dtype)
            _, ys = jax.lax.scan(step, h0, xs.T)
            ys = jnp.transpose(ys, (1, 0, 2))
            KX = M.shape[1]
            M2 = M[:, :, 0]
            shifts = jnp.stack([jnp.pad(xs, ((0, 0), (j, 0)))[:, :L] for j in range(KX)], axis=-1)
            return ys + jnp.einsum('nlj,oj->nlo', shifts, M2)
        key = jax.random.key(seed)
        ks = jax.random.split(key, 7)
        BSZ, L, D, S, KX = (4, 256, 64, 64, 8)
        x = jax.random.normal(ks[0], (BSZ, L, D), jnp.float32)
        A = 0.9 + 0.099 * jax.random.uniform(ks[1], (S,), jnp.float32)
        Bv = 0.1 * jax.random.normal(ks[2], (S,), jnp.float32)
        C = 0.1 * jax.random.normal(ks[3], (S, 2 * K), jnp.float32)
        M = 0.1 * jax.random.normal(ks[4], (2 * K, KX, 1), jnp.float32)
        M_phi_plus = 0.02 * jax.random.normal(ks[5], (K, D, D), jnp.float32)
        M_phi_minus = 0.02 * jax.random.normal(ks[6], (K, D, D), jnp.float32)
        return dict(x=x, A=A, Bv=Bv, C=C, M=M, M_phi_plus=M_phi_plus, M_phi_minus=M_phi_minus)
    _L1_attn_all = _L1_attn_setup()
    _L1_attn_in = {k: v for k, v in _L1_attn_all.items() if k in ('A', 'Bv', 'C', 'M', 'M_phi_plus', 'M_phi_minus')}
    del _L1_attn_all

    def _L1_ffn_setup():
        import jax, jax.numpy as jnp
        import numpy as np
        E, D, H, TOP_K = (6, 64, 64, 2)
        ROUTER_H = D // 2
        key = jax.random.key(seed)
        ks = jax.random.split(key, 12)
        s = 1.0 / np.sqrt(D)
        sh = 1.0 / np.sqrt(H)
        sr = 1.0 / np.sqrt(ROUTER_H)
        return {'features': jax.random.normal(ks[0], (8, 1024, D), dtype=jnp.float32), 'router_w1': jax.random.uniform(ks[1], (D, ROUTER_H), jnp.float32, -s, s), 'router_b1': jnp.zeros((ROUTER_H,), jnp.float32), 'router_w2': jax.random.uniform(ks[2], (ROUTER_H, E), jnp.float32, -sr, sr), 'router_b2': jnp.zeros((E,), jnp.float32), 'expert_w1': jax.random.uniform(ks[3], (E, D, H), jnp.float32, -s, s), 'expert_b1': jnp.zeros((E, H), jnp.float32), 'expert_w2': jax.random.uniform(ks[4], (E, H, H), jnp.float32, -sh, sh), 'expert_b2': jnp.zeros((E, H), jnp.float32), 'expert_w3': jax.random.uniform(ks[5], (E, H, D), jnp.float32, -sh, sh), 'expert_b3': jnp.zeros((E, D), jnp.float32)}
    _L1_ffn_all = _L1_ffn_setup()
    _L1_ffn_in = {k: v for k, v in _L1_ffn_all.items() if k in ('router_w1', 'router_b1', 'router_w2', 'router_b2', 'expert_w1', 'expert_b1', 'expert_w2', 'expert_b2', 'expert_w3', 'expert_b3')}
    del _L1_ffn_all
    return {'x': x, 'txt': txt, 'L0_tok_W': _L0_tok_in['W'], 'L0_attn_pre_g': _L0_attn_in['pre_g'], 'L0_attn_pre_b': _L0_attn_in['pre_b'], 'L0_attn_post_g': _L0_attn_in['post_g'], 'L0_attn_post_b': _L0_attn_in['post_b'], 'L0_attn_norm_w': _L0_attn_in['norm_w'], 'L0_attn_inproj_w': _L0_attn_in['inproj_w'], 'L0_attn_conv_w': _L0_attn_in['conv_w'], 'L0_attn_conv_b': _L0_attn_in['conv_b'], 'L0_attn_xproj_w': _L0_attn_in['xproj_w'], 'L0_attn_dtproj_w': _L0_attn_in['dtproj_w'], 'L0_attn_dtproj_b': _L0_attn_in['dtproj_b'], 'L0_attn_A_log': _L0_attn_in['A_log'], 'L0_attn_D_param': _L0_attn_in['D_param'], 'L0_attn_outproj_w': _L0_attn_in['outproj_w'], 'L0_attn_normf_w': _L0_attn_in['normf_w'], 'L0_ffn_gamma': _L0_ffn_in['gamma'], 'L0_ffn_beta': _L0_ffn_in['beta'], 'L0_ffn_Wr': _L0_ffn_in['Wr'], 'L0_ffn_br': _L0_ffn_in['br'], 'L0_ffn_W1': _L0_ffn_in['W1'], 'L0_ffn_b1': _L0_ffn_in['b1'], 'L0_ffn_W2': _L0_ffn_in['W2'], 'L0_ffn_b2': _L0_ffn_in['b2'], 'L1_attn_A': _L1_attn_in['A'], 'L1_attn_Bv': _L1_attn_in['Bv'], 'L1_attn_C': _L1_attn_in['C'], 'L1_attn_M': _L1_attn_in['M'], 'L1_attn_M_phi_plus': _L1_attn_in['M_phi_plus'], 'L1_attn_M_phi_minus': _L1_attn_in['M_phi_minus'], 'L1_ffn_router_w1': _L1_ffn_in['router_w1'], 'L1_ffn_router_b1': _L1_ffn_in['router_b1'], 'L1_ffn_router_w2': _L1_ffn_in['router_w2'], 'L1_ffn_router_b2': _L1_ffn_in['router_b2'], 'L1_ffn_expert_w1': _L1_ffn_in['expert_w1'], 'L1_ffn_expert_b1': _L1_ffn_in['expert_b1'], 'L1_ffn_expert_w2': _L1_ffn_in['expert_w2'], 'L1_ffn_expert_b2': _L1_ffn_in['expert_b2'], 'L1_ffn_expert_w3': _L1_ffn_in['expert_w3'], 'L1_ffn_expert_b3': _L1_ffn_in['expert_b3']}

def reference(x, txt, L0_tok_W, L0_attn_pre_g, L0_attn_pre_b, L0_attn_post_g, L0_attn_post_b, L0_attn_norm_w, L0_attn_inproj_w, L0_attn_conv_w, L0_attn_conv_b, L0_attn_xproj_w, L0_attn_dtproj_w, L0_attn_dtproj_b, L0_attn_A_log, L0_attn_D_param, L0_attn_outproj_w, L0_attn_normf_w, L0_ffn_gamma, L0_ffn_beta, L0_ffn_Wr, L0_ffn_br, L0_ffn_W1, L0_ffn_b1, L0_ffn_W2, L0_ffn_b2, L1_attn_A, L1_attn_Bv, L1_attn_C, L1_attn_M, L1_attn_M_phi_plus, L1_attn_M_phi_minus, L1_ffn_router_w1, L1_ffn_router_b1, L1_ffn_router_w2, L1_ffn_router_b2, L1_ffn_expert_w1, L1_ffn_expert_b1, L1_ffn_expert_w2, L1_ffn_expert_b2, L1_ffn_expert_w3, L1_ffn_expert_b3):
    import jax
    import jax.numpy as jnp

    def _L0_tok_ref(x, W):
        import jax, jax.numpy as jnp
        import numpy as np
        PATCH_LEN = 16
        STRIDE = 8
        PAD = 8
        B, C, T, V = x.shape
        xp = jnp.pad(x, ((0, 0), (0, 0), (0, PAD), (0, 0)), mode='edge')
        Tp = T + PAD
        N = (Tp - PATCH_LEN) // STRIDE + 1
        idx = jnp.arange(N)[:, None] * STRIDE + jnp.arange(PATCH_LEN)[None, :]
        patches = xp[:, :, idx, :]
        patches = jnp.transpose(patches, (0, 4, 2, 3, 1))
        xf = jnp.fft.rfft(patches, axis=-2, norm='ortho')
        F = xf.shape[-2]
        x_real = xf.real.reshape(B, V, N, F * C)
        x_imag = xf.imag.reshape(B, V, N, F * C)
        x_emb = jnp.concatenate([x_real, x_imag], axis=-1)
        x_emb = x_emb @ W.T
        return x_emb.reshape(B, V * N, -1)

    def _L0_attn_ref(x, pre_g, pre_b, post_g, post_b, norm_w, inproj_w, conv_w, conv_b, xproj_w, dtproj_w, dtproj_b, A_log, D_param, outproj_w, normf_w):
        import jax, jax.numpy as jnp
        import numpy as np
        B, T, H, D, N, R, K = (2, 256, 64, 256, 16, 16, 4)
        EPS = 1e-05

        def layer_norm(x, g, b):
            m = jnp.mean(x, -1, keepdims=True)
            v = jnp.mean((x - m) ** 2, -1, keepdims=True)
            return (x - m) * jax.lax.rsqrt(v + EPS) * g + b

        def rms_norm(x, w):
            return x * jax.lax.rsqrt(jnp.mean(x * x, -1, keepdims=True) + EPS) * w

        def selective_scan(u, dt, A, Bm, Cm, Dp):
            dA = jnp.exp(dt[..., None] * A)
            dBu = (dt * u)[..., None] * Bm[:, :, None, :]

            def step(h, inp):
                dA_t, dBu_t, C_t = inp
                h = dA_t * h + dBu_t
                return (h, jnp.einsum('bdn,bn->bd', h, C_t))
            h0 = jnp.zeros((u.shape[0], u.shape[2], A.shape[1]), u.dtype)
            _, ys = jax.lax.scan(step, h0, (dA.swapaxes(0, 1), dBu.swapaxes(0, 1), Cm.swapaxes(0, 1)))
            return ys.swapaxes(0, 1) + u * Dp

        def mamba_mixer(h, inproj_w, conv_w, conv_b, xproj_w, dtproj_w, dtproj_b, A_log, Dp, outproj_w):
            proj = jnp.einsum('bth,eh->bte', h, inproj_w)
            u, gate = (proj[..., :D], proj[..., D:])
            uc = jax.lax.conv_general_dilated(u.swapaxes(1, 2), conv_w, (1,), [(K - 1, 0)], dimension_numbers=('NCH', 'OIH', 'NCH'), feature_group_count=D)
            u = jax.nn.silu(uc + conv_b[None, :, None]).swapaxes(1, 2)
            ssm = jnp.einsum('btd,ed->bte', u, xproj_w)
            dt_r, Bm, Cm = (ssm[..., :R], ssm[..., R:R + N], ssm[..., R + N:])
            dt = jax.nn.softplus(jnp.einsum('btr,dr->btd', dt_r, dtproj_w) + dtproj_b)
            A = -jnp.exp(A_log)
            y = selective_scan(u, dt, A, Bm, Cm, Dp)
            y = y * jax.nn.silu(gate)
            return jnp.einsum('btd,hd->bth', y, outproj_w)

        def _forward(x, pre_g, pre_b, post_g, post_b, norm_w, inproj_w, conv_w, conv_b, xproj_w, dtproj_w, dtproj_b, A_log, D_param, outproj_w, normf_w):
            h = layer_norm(x, pre_g, pre_b)
            for i in range(2):
                h = h + mamba_mixer(rms_norm(h, norm_w[i]), inproj_w[i], conv_w[i], conv_b[i], xproj_w[i], dtproj_w[i], dtproj_b[i], A_log[i], D_param[i], outproj_w[i])
            h = rms_norm(h, normf_w)
            return layer_norm(h, post_g, post_b)
        return _forward(x, pre_g, pre_b, post_g, post_b, norm_w, inproj_w, conv_w, conv_b, xproj_w, dtproj_w, dtproj_b, A_log, D_param, outproj_w, normf_w)

    def _L0_ffn_ref(x, gamma, beta, Wr, br, W1, b1, W2, b2):
        import jax, jax.numpy as jnp
        import numpy as np
        E = 8
        K = 2
        D = 64
        H = 128
        DOUT = 64
        EPS = 1e-05
        mu = jnp.mean(x, axis=-1, keepdims=True)
        var = jnp.mean(jnp.square(x - mu), axis=-1, keepdims=True)
        xn = (x - mu) * jax.lax.rsqrt(var + EPS) * gamma + beta
        logits = jnp.einsum('bsd,de->bse', xn, Wr) + br
        top_vals, top_idx = jax.lax.top_k(logits, K)
        w = jax.nn.softmax(top_vals, axis=-1)
        w_full = jnp.einsum('bsk,bske->bse', w, jax.nn.one_hot(top_idx, E, dtype=w.dtype))
        y = jnp.zeros(x.shape[:-1] + (DOUT,), x.dtype)
        for e in range(E):
            h = jax.nn.gelu(jnp.einsum('bsd,dh->bsh', xn, W1[e]) + b1[e], approximate=False)
            y_e = jnp.einsum('bsh,hd->bsd', h, W2[e]) + b2[e]
            y = y + y_e * w_full[..., e, None]
        return y

    def _L1_attn_ref(x, A, Bv, C, M, M_phi_plus, M_phi_minus):
        import jax, jax.numpy as jnp
        import numpy as np
        K = 24

        def _lds(xs, A, Bv, C, M):
            N, L = xs.shape
            S = A.shape[0]

            def step(h, xt):
                h = h * A[None, :] + xt[:, None] * Bv[None, :]
                return (h, h @ C)
            h0 = jnp.zeros((N, S), xs.dtype)
            _, ys = jax.lax.scan(step, h0, xs.T)
            ys = jnp.transpose(ys, (1, 0, 2))
            KX = M.shape[1]
            M2 = M[:, :, 0]
            shifts = jnp.stack([jnp.pad(xs, ((0, 0), (j, 0)))[:, :L] for j in range(KX)], axis=-1)
            return ys + jnp.einsum('nlj,oj->nlo', shifts, M2)
        bsz, L, D = x.shape
        xr = jnp.transpose(x, (0, 2, 1)).reshape(bsz * D, L)
        U = _lds(xr, A, Bv, C, M)
        U = U.reshape(bsz, D, L, 2 * K)
        U = jnp.transpose(U, (0, 2, 3, 1))
        spectral_plus = jnp.einsum('blkd,kde->ble', U[:, :, :K, :], M_phi_plus)
        spectral_minus = jnp.einsum('blkd,kde->ble', U[:, :, K:, :], M_phi_minus)
        return spectral_plus + spectral_minus

    def _L1_ffn_ref(features, router_w1, router_b1, router_w2, router_b2, expert_w1, expert_b1, expert_w2, expert_b2, expert_w3, expert_b3):
        import jax, jax.numpy as jnp
        import numpy as np
        E, D, H, TOP_K = (6, 64, 64, 2)
        ROUTER_H = D // 2
        rh = jax.nn.relu(features @ router_w1 + router_b1)
        expert_logits = jax.nn.softmax(rh @ router_w2 + router_b2, axis=-1)
        top_w, top_i = jax.lax.top_k(expert_logits, TOP_K)
        routing_weights = jax.nn.softmax(top_w, axis=-1)
        h1 = jax.nn.relu(jnp.einsum('bsd,edh->bseh', features, expert_w1) + expert_b1)
        h2 = jax.nn.relu(jnp.einsum('bseh,ehf->bsef', h1, expert_w2) + expert_b2)
        expert_out = jnp.einsum('bsef,efo->bseo', h2, expert_w3) + expert_b3
        sel = jnp.take_along_axis(expert_out, top_i[:, :, :, None], axis=2)
        combined = jnp.sum(sel * routing_weights[..., None], axis=2)
        return combined
    h = _L0_tok_ref(x, L0_tok_W)
    h = jnp.concatenate([h, txt], axis=1)
    h = h + _L0_attn_ref(_layernorm(h, axis=-1), L0_attn_pre_g, L0_attn_pre_b, L0_attn_post_g, L0_attn_post_b, L0_attn_norm_w, L0_attn_inproj_w, L0_attn_conv_w, L0_attn_conv_b, L0_attn_xproj_w, L0_attn_dtproj_w, L0_attn_dtproj_b, L0_attn_A_log, L0_attn_D_param, L0_attn_outproj_w, L0_attn_normf_w)
    h = h + _L0_ffn_ref(_layernorm(h, axis=-1), L0_ffn_gamma, L0_ffn_beta, L0_ffn_Wr, L0_ffn_br, L0_ffn_W1, L0_ffn_b1, L0_ffn_W2, L0_ffn_b2)
    h = h + _L1_attn_ref(_layernorm(h, axis=-1), L1_attn_A, L1_attn_Bv, L1_attn_C, L1_attn_M, L1_attn_M_phi_plus, L1_attn_M_phi_minus)
    h = h + _L1_ffn_ref(_layernorm(h, axis=-1), L1_ffn_router_w1, L1_ffn_router_b1, L1_ffn_router_w2, L1_ffn_router_b2, L1_ffn_expert_w1, L1_ffn_expert_b1, L1_ffn_expert_w2, L1_ffn_expert_b2, L1_ffn_expert_w3, L1_ffn_expert_b3)
    return h

_drawn_inputs = setup_inputs


def setup_inputs(seed=0):
    import zlib

    import numpy as np

    out = dict(_drawn_inputs(seed))
    spreads = {'L0_attn_pre_g': (1.0, 0.2),
     'L0_attn_pre_b': (0.0, 0.1),
     'L0_attn_post_g': (1.0, 0.2),
     'L0_attn_post_b': (0.0, 0.1),
     'L0_attn_norm_w': (1.0, 0.6),
     'L0_attn_conv_b': (0.0, 0.726),
     'L0_attn_D_param': (1.0, 0.6),
     'L0_attn_normf_w': (1.0, 0.2),
     'L0_ffn_br': (0.0, 0.1),
     'L1_ffn_router_b1': (0.0, 0.917),
     'L1_ffn_router_b2': (0.0, 1.373),
     'L1_ffn_expert_b1': (0.0, 2.0),
     'L1_ffn_expert_b2': (0.0, 1.895),
     'L1_ffn_expert_b3': (0.0, 0.718)}
    factors = {'L0_attn_inproj_w': 5.887,
     'L0_attn_conv_w': 8.0,
     'L0_attn_xproj_w': 8.0,
     'L0_attn_dtproj_w': 8.0,
     'L0_attn_dtproj_b': 8.0,
     'L0_attn_A_log': 8.0,
     'L0_attn_outproj_w': 4.952,
     'L0_ffn_gamma': 8.0,
     'L0_ffn_beta': 8.0,
     'L0_ffn_Wr': 8.0,
     'L0_ffn_W1': 5.834,
     'L0_ffn_b1': 8.0,
     'L0_ffn_W2': 4.734,
     'L0_ffn_b2': 8.0,
     'L1_ffn_expert_w1': 5.375,
     'L1_ffn_expert_w2': 2.815}
    for name, (base, spread) in spreads.items():
        noise = np.random.default_rng([zlib.crc32(name.encode()), seed]).standard_normal(out[name].shape)
        drawn = base * np.exp(spread * noise) if base else spread * noise
        out[name] = jnp.asarray(drawn.astype(out[name].dtype))
    for name, factor in factors.items():
        out[name] = (out[name] * factor).astype(out[name].dtype)
    return out
```

```python
import concourse.bass as bass
import concourse.mybir as mybir
import numpy as np
from contextlib import ExitStack

BATCH, CH, TIME, VARS = 4, 64, 128, 64
TXT = 77
PATCH, STRIDE = 16, 8
NPATCH = (TIME + STRIDE - PATCH) // STRIDE + 1
FREQ = PATCH // 2 + 1
F = 64
TOK = VARS * NPATCH + TXT
CHK = 3
TC = TOK // CHK
PAIRCOLS = 2 * TOK
TILES = -(-PAIRCOLS // 128)
PADCOLS = TILES * 128
EPS = 1e-5
D, NS, R, KC = 256, 16, 16, 4
LAYERS = 2
SLOTS = BATCH * CHK
SW = TC + 4
E0, HID0 = 8, 128
SS, KF, KX = 64, 24, 8
CL = 8
NCH = -(-TOK // CL)
AW = CL - 1 + NCH * CL + 1
E1N, RH = 6, 32
XW = (TIME + STRIDE) // 2 * VARS
UW = 2 * TC
BIG = 1e30
SERIES_BELOW = 1.0 / 64
PD = 12
SKIP_AT = 7
POOL_GATE_AT = 5
PE_PIECE_AT, ACT_PIECE_AT, DVE_PIECE_AT = (1, 3, 5), (2, 4, 6, 8, 11), (7, 14, 18, 24, 26, 28)
V_PREG, V_PREB, V_POSTG, V_POSTB, V_NFW, V_G0, V_B0, V_RB1, V_A, V_BV = range(10)
M_CB, M_DTB, M_D, M_NW, M_A = 0, 2, 4, 6, 7
MCOLS = M_A + 2 * NS
W_U, W_G, W_X, W_DT, W_O, W_C = 0, 512, 768, 1024, 1280, 1664
W_SIZE = W_C + MCOLS + 1
V_EPS, V_EPS2 = 10, 11
V_SIZE = 12
C_SIZE = 416 + V_SIZE
E0_SIZE, E1_SIZE, ATT_SIZE = 2728, 3365, 400


def fusion_program(nc, t):
    fp32, bf16 = mybir.dt.float32, mybir.dt.bfloat16
    ALU, ACT, AX = mybir.AluOpType, mybir.ActivationFunctionType, mybir.AxisListType
    ds = bass.ds
    ctx = ExitStack()
    with ctx:
        def sb(name, shape, dt=fp32):
            return ctx.enter_context(nc.sbuf_tensor(name, shape, dt))

        def sem(name):
            return ctx.enter_context(nc.semaphore(name))

        H = sb("H", [128, PAIRCOLS])
        Z = sb("Z", [128, PADCOLS])
        big1 = sb("big1", [128, (2 * SLOTS + 1) * UW])
        X = big1[:, 0:BATCH * XW].rearrange("p (b m) -> p b m", b=BATCH)
        U = big1[:, 0:(SLOTS + 1) * UW]
        SG = big1[:, (SLOTS + 1) * UW:]
        QB = big1[:, 0:2 * F * SS].rearrange("p (s q e) -> p s q e", s=SS, q=2)
        ZS = big1[:, 2 * F * SS:(2 * F + NCH) * SS].rearrange("p (c s) -> p c s", s=SS)
        big2 = sb("big2", [128, NCH * 128])
        HB = big2[:, 0:2 * NS * TC].rearrange("p (j t) -> p j t", j=2 * NS)
        cut = [2 * NS * TC]

        def scan_buffer(n):
            cut[0] += n
            return big2[:, cut[0] - n:cut[0]]
        dbu = [scan_buffer(TC) for _ in range(3)] + [None]
        csb = [scan_buffer(TC) for _ in range(2)]
        prod = [scan_buffer(TC) for _ in range(3)] + [None]
        ssmf = scan_buffer(TC)
        bcs = [scan_buffer(184).bitcast(bf16)[:, 0:TC] for _ in range(2)]
        dt_ = [scan_buffer(UW) for _ in range(2)]
        dtu = [scan_buffer(UW), sb("dtu1", [128, UW])[:, :]]
        SH = big2[:, :].rearrange("p (b s c) -> p b s c", b=2, s=SS)
        ZT = big2[:, :].rearrange("p (b g m) -> p b g m", b=2, m=128)
        hn2 = sb("hn2", [128, max(SLOTS * SW, BATCH * AW)])
        LG = hn2[:, 0:AW * BATCH].rearrange("p (q b w) -> p q b w", q=2, b=2)
        nb = sb("nb", [128, 9 * TC])
        sq = [nb[:, i * TC:(i + 1) * TC] for i in range(3)]
        lnv = [nb[:, (3 + i) * TC:(4 + i) * TC] for i in range(3)]
        rstd = [nb[:, (6 + i) * TC:(7 + i) * TC] for i in range(3)]
        sqz = [big2[:, i * TC:(i + 1) * TC] for i in range(3)]
        y1 = nb[:, 0:UW]
        xdt = nb[:, 3 * TC:3 * TC + UW]
        spl = nb[:, 6 * TC:6 * TC + UW]
        res = nb[:, 5 * TC:6 * TC]
        prod[3], dbu[3] = nb[:, 2 * TC:3 * TC], nb[:, 8 * TC:9 * TC]
        cst = sb("cst", [128, C_SIZE])
        ident, center, mean = (cst[:, 128 * i:128 * i + 128] for i in range(3))
        selc, vec = cst[:, 384:416], cst[:, 416:416 + V_SIZE]
        ringc = sb("ringc", [128, 32])
        diag = sb("diag", [128, 2, 128])
        centerw, meaneps = diag[:, 0, :], diag[:, 1, :]
        sel = sb("sel", [128, 32], bf16)
        mw = [sb(f"mw{l}", [128, W_SIZE]) for l in range(LAYERS)]
        psum = ctx.enter_context(nc.psum_tensor("psum", [128, 4096], fp32))

        e0 = big1[:, 0:E0_SIZE]
        w1z = big1[:, 0:2048].rearrange("p (e q h) -> p e q h", e=E0, q=2)
        w2s = big1[:, 2048:2560].rearrange("p (e f) -> p e f", e=E0)
        wr0, b1c = big1[:, 2560:2576], big1[:, 2576:2584]
        br0 = big1[:, 2584:2592]
        idx0, b2bd = big1[:, 2592:2600], big1[:, 2600:2728]
        hid = [big2[:, 1101 + i * TC:1101 + (i + 1) * TC] for i in range(4)]
        hsc = [big2[:, 2569 + i * TC:2569 + (i + 1) * TC] for i in range(4)]
        wtok = big2[:, 4096:4096 + PADCOLS].rearrange("p (g c) -> p g c", g=TILES)
        wtf = big2[:, 6400:6400 + PADCOLS]
        wres = big2[:, 8704:8704 + PADCOLS]
        wtb = big2[:, 11008:11008 + PADCOLS // 2].bitcast(bf16)
        rhid = big2[:, 12160:12160 + PADCOLS]
        rt = big2[:, 14464:14464 + 2600]
        w123 = big1[:, 0:2304].rearrange("p (k e m) -> p k e m", k=3, e=E1N)
        rw1, rw2 = big1[:, 2304:2432], big1[:, 2432:2444]
        br1, idx1 = big1[:, 2444:2450], big1[:, 2450:2456]
        rb1, eb12 = big1[:, 2456:2457], big1[:, 2457:2469]
        b3bd, sel2f = big1[:, 2469:2597], big1[:, 2597:3365]
        sel2 = big1[:, 3365:3749].bitcast(bf16).rearrange("p (e m) -> p e m", e=E1N)
        mphi = big1[0:48, 14254:18350]
        wv = mw[0][:, 0:1024].rearrange("p (c s) -> p c s", c=16)
        attc = mw[0][:, 1024:1024 + ATT_SIZE]
        cs, ct, m2 = attc[0:64, 0:48], attc[0:48, 48:112], attc[0:48, 112:120]
        cmask, acol, bcol = attc[:, 120:136], attc[:, 136:137], attc[:, 137:138]
        pw, ab, abr = attc[:, 138:147], attc[:, 147:155], attc[:, 155:163]
        abrep = attc[0:64, 163:291]
        gk = attc[0:48, 291:307].rearrange("p (q j) -> p q j", q=2)
        gfull = attc[0:48, 307:315]
        a8row, apair = attc[:, 315:379], attc[:, 379:395]
        kf, km, kx = (mw[1][:, 256 * i:256 * i + 256].rearrange("p (m e) -> p m e", m=4)
                      for i in range(3))
        xt = nb[:, 0:2304].rearrange("p (k b q d) -> p k b q d", k=9, b=2, q=2)

        def wu(l):
            return mw[l][:, W_U:W_U + 512].rearrange("p (k d) -> p k d", k=2)

        def wx(l):
            return mw[l][:, W_X:W_X + 256].rearrange("p (k m) -> p k m", k=2)

        def wo(l, half, par):
            at = W_O + 192 * half + 64 * (1 - par)
            return mw[l][:, at:at + 128]

        def bank(i, n=TC):
            return psum[:, 512 * i:512 * i + n]

        def col(l, i):
            return mw[l][:, W_C + i:W_C + i + 1]

        wt18 = big2[0:18, 0:4096].rearrange("p (f c) -> p f c", f=F)
        dftm = big2[0:18, 4096:4096 + PATCH]
        gt = big2[:, 4608:5120].rearrange("p (j f) -> p j f", j=8)
        inp = [big2[:, 5120 + 1024 * l:5632 + 1024 * l] for l in range(LAYERS)]
        cwt = [big2[:, 5632 + 1024 * l:6144 + 1024 * l].rearrange("p (k d) -> p k d", k=2)
               for l in range(LAYERS)]

        block = ctx.enter_context(nc.Block())
        setup_loaded, xload = sem("setup_loaded"), [sem(f"xload{b}") for b in range(BATCH)]
        zeroed = sem("zeroed")
        patch_w_ready, patch_w_copied = sem("patch_w_ready"), sem("patch_w_copied")
        embedded, h_ready = sem("embedded"), sem("h_ready")
        a_exp, scaled, zsq, shifted, mats_ready, tap_step, sp_exp, sp_ln = (
            sem(n) for n in ("a_exp", "scaled", "zsq", "shifted", "mats_ready", "tap_step",
                             "sp_exp", "sp_ln"))
        spare = sem("spare")
        e0_loaded, e1_loaded, att_loaded = sem("e0_loaded"), sem("e1_loaded"), sem("att_loaded")
        logits, wtok_ready, wt_mm, wt_copied, wt_cast = (sem(n) for n in (
            "logits", "wtok_ready", "wt_mm", "wt_copied", "wt_cast"))
        wt_split, r_step, r_exp, wtok_zero = (sem(n) for n in (
            "wt_split", "r_step", "r_exp", "wtok_zero"))
        h1_ready, gelu_done, wrep, hs_done, e_out, h_e0 = (sem(n) for n in (
            "h1_ready", "gelu_done", "wrep", "hs_done", "e_out", "h_e0"))
        l1_ready, a1_done, l2_ready, a2_done, wrep1, hs1_done, e1_out, h_e1 = (sem(n) for n in (
            "l1_ready", "a1_done", "l2_ready", "a2_done", "wrep1", "hs1_done", "e1_out", "h_e1"))
        rh_mm, rh_done, lg_zero, lg_ready = (sem(n) for n in (
            "rh_mm", "rh_done", "lg_zero", "lg_ready"))
        g_mm, g_ready, kj_mm, kj_ready, p_mm, wv_ready = (sem(n) for n in (
            "g_mm", "g_ready", "kj_mm", "kj_ready", "p_mm", "wv_ready"))
        qb_zero, q_mm, q_even, q_odd = (sem(n) for n in ("qb_zero", "q_mm", "q_even", "q_odd"))
        a_step, xt_mm, xt_ready, v_mm, v_copied, state_done, taps_mm, z_mm, z_copied = (
            sem(n) for n in ("a_step", "xt_mm", "xt_ready", "v_mm", "v_copied", "state_done",
                             "taps_mm", "z_mm", "z_copied"))
        zt_mm, zt_copied, f_out, h_att = (sem(n) for n in ("zt_mm", "zt_copied", "f_out", "h_att"))
        sel2_ready = sem("sel2_ready")
        T_SMALL = 1500
        centered, squared, var_ready = sem("centered"), sem("squared"), sem("var_ready")
        ln_done, rstd_ready, normed = sem("ln_done"), sem("rstd_ready"), sem("normed")
        dve_step = sem("dve_step")
        proj_ready, silu_done = sem("proj_ready"), sem("silu_done")
        outp_ready, z_updated = sem("outp_ready"), sem("z_updated")
        pre_mm, pre_act, bc_cast, pre_dve = sem("pre_mm"), sem("pre_act"), sem("bc_cast"), sem("pre_dve")
        brep, crep, ccopied = sem("brep"), sem("crep"), sem("ccopied")
        da_ready, dbu_done, scanned = sem("da_ready"), sem("dbu_done"), sem("scanned")
        hc_done, y_acc, y_out, gated = sem("hc_done"), sem("y_acc"), sem("y_out"), sem("gated")
        stored = sem("stored")
        CR_SCAN, CR_DBU, CR_HC, CR_YACC, CR_CC, CR_YOUT = 4, 4, 4, 4, 2, 3
        SETUP = 16 * 6
        t["r_soft"], t["r_top"] = 20 + 3, (14, 20 + 19)


        @block.sync
        def _(sp):
            for dst, src in ((cst[:, :], t["cst"]), (big2[0:18, 0:4096 + PATCH], t["w18"]),
                             (big2[:, 5120:7168], t["inp"]), (mw[0][:, :], t["mw0"]),
                             (mw[1][:, :], t["mw1"])):
                sp.dma_start(dst, src).then_inc(setup_loaded, 16)
            sp.dma_start(H[:, :].rearrange("p (b t) -> p b t", b=2)[:, :, VARS * NPATCH:],
                         t["txt"].rearrange("p (b t) -> p b t", b=2)).then_inc(setup_loaded, 16)
            for b in range(BATCH):
                sp.dma_start(X[:, b, :], t["x"][:, b * XW:(b + 1) * XW]).then_inc(xload[b], 16)
            sp.wait_ge(z_updated, 15)
            sp.dma_start(e0, t["e0"]).then_inc(e0_loaded, 16)
            sp.dma_start(mphi, t["mphi"]).then_inc(att_loaded, 16)
            sp.dma_start(attc[:, 0:138], t["att"]).then_inc(att_loaded, 16)
            sp.wait_ge(z_mm, SS)
            sp.dma_start(big1[:, 0:E1_SIZE], t["e1"]).then_inc(e1_loaded, 16)
            sp.wait_ge(h_e1, 8)
            sp.dma_start(t["out"], H[:, :]).then_inc(stored, 16)
            sp.wait_ge(stored, 16)

        def scan_pool(pool, l):
            with pool.Fori(0, 2) as bp:
                for si in range(6):
                    s = 6 * bp + si
                    S = 12 * l + s
                    for j in range(2 * NS):
                        n = j // 2
                        if j % 2 == 0:
                            pool.wait_ge(ccopied, 193 * l + 16 * s + n + 1 + CR_CC)
                        pool.wait_ge(y_acc, 32 * S + j - 3 + CR_YACC)
                        pool.wait_ge(scanned, 32 * S + 2 * l + j + 1 + CR_SCAN)
                        nc.gpsimd.tensor_tensor(prod[j % 4], HB[:, j, :], csb[n % 2],
                                                ALU.mult).then_inc(hc_done, 1)
                        if j == POOL_GATE_AT:
                            pool.wait_ge(y_out, 2 * S + CR_YOUT)
                            g = big1[:, ds((SLOTS + s) * UW, UW)]
                            nc.gpsimd.tensor_tensor(g, g, y1, ALU.mult).then_inc(gated, 1)
            pool.wait_ge(y_out, 24 * (l + 1) + CR_YOUT)
            g = SG[:, 11 * UW:12 * UW]
            nc.gpsimd.tensor_tensor(g, g, y1, ALU.mult).then_inc(gated, 1)

        @block.gpsimd
        def _(pool):
            nc.gpsimd.memset(hn2[:, :], 0.0).then_inc(zeroed, 1)
            nc.gpsimd.memset(Z[:, PAIRCOLS:], 0.0).then_inc(zeroed, 1)
            for l in range(LAYERS):
                scan_pool(pool, l)
            pool.wait_ge(z_updated, 15)
            nc.gpsimd.memset(wtok, 0.0).then_inc(wtok_zero, 1)
            nc.gpsimd.memset(hn2[:, 0:BATCH * AW], 0.0).then_inc(lg_zero, 1)
            pool.wait_ge(h_e0, 8)
            nc.gpsimd.memset(big1[:, 0:2 * F * SS], 0.0).then_inc(qb_zero, 1)
            pool.wait_ge(h_att, 22)
            nc.gpsimd.memset(wtok, 0.0).then_inc(wtok_zero, 1)

        def norm_pe(pe, cn, rn, cmat, src, extra, emat):
            with pe.Fori(0, 2) as bp:
                for c in range(3):
                    pe.wait_ge(normed, 6 * cn + 3 * bp + c + 1)
                    nc.tensor.matmul(bank(c), cmat, src[:, ds(bp * TOK + c * TC, TC)],
                                     start=True, stop=True).then_inc(centered, 1)
                for c in range(3):
                    pe.wait_ge(squared, 6 * rn + 3 * bp + c + 1)
                    last = nc.tensor.matmul(bank(3 + c), mean, sq[c], start=True,
                                            stop=extra is None)
                    if extra is not None:
                        pe.wait_ge(zsq, 3 * bp + c + 1)
                        last = nc.tensor.matmul(bank(3 + c), emat, extra[c], start=False, stop=True)
                    last.then_inc(var_ready, 1)

        def rms_pe(pe, l):
            use = 1 + l
            with pe.Fori(0, 2) as bp:
                g = 6 * use + 3 * bp
                for c in range(3):
                    pe.wait_ge(squared, g + c + 1)
                    nc.tensor.matmul(bank(3 + c), mean, sq[c], start=True,
                                     stop=True).then_inc(var_ready, 1)
                for c in range(3):
                    pe.wait_ge(tap_step, 32 * l + 16 * bp + (4, 10, 16)[c])
                    for par in range(2):
                        slot = 6 * bp + 3 * par + c
                        for w in range(4):
                            i = 8 * c + 4 * par + w
                            pe.wait_ge(silu_done, 48 * l + 24 * bp + i + 1)
                            half, steps = w % 2, (2 if w < 2 else 1)
                            for k in range(steps):
                                wt = (wu(l)[:, k, 128 * half:128 * half + 128] if w < 2 else
                                      mw[l][:, W_G + 128 * half:W_G + 128 * half + 128])
                                last = nc.tensor.matmul(bank(6 + w % 2), wt,
                                                        hn2[:, ds(slot * SW + 3 - 2 * k, TC)],
                                                        start=(k == 0), stop=(k == steps - 1))
                            last.then_inc(proj_ready, 1)

        def pre_pe(pe, l, slot, piece):
            p = 13 * l + slot
            if piece == 0:
                pe.wait_ge(pre_act, 3 * p + 1)
                for k in range(2):
                    last = nc.tensor.matmul(bank(7), wx(l)[:, k, :],
                                            U[:, ds(slot * UW + k * TC, TC)],
                                            start=(k == 0), stop=(k == 1))
            else:
                pe.wait_ge(pre_act, 3 * p + piece + 1)
                if piece == 1:
                    pe.wait_ge(bc_cast, p + 1)
                last = nc.tensor.matmul(
                    bank(7), mw[l][:, W_DT + 128 * (piece - 1):W_DT + 128 * piece], ssmf,
                    start=True, stop=True)
            last.then_inc(pre_mm, 1)

        def rep_b(pe, l, s, n, q):
            S = 12 * l + s
            pe.wait_ge(dbu_done, 32 * S + 2 * n - 2 + CR_DBU)
            if n == 0 or n == NS:
                pe.wait_ge(pre_dve, PD * (13 * l + s + (n // NS)) + 4)
            q = (q + n // NS) % 2
            nc.tensor.matmul(bank(2 + n % 2), sel[:, n % NS:n % NS + 1].broadcast_to([128, 128]),
                             bcs[q], start=True, stop=True).then_inc(brep, 1)

        def rep_c(pe, l, s, n, q):
            pe.wait_ge(ccopied, 193 * l + 16 * s + n + CR_CC)
            q = (q + n // NS) % 2
            m = NS + n % NS
            nc.tensor.matmul(bank(4), sel[:, m:m + 1].broadcast_to([128, 128]),
                             bcs[q], start=True, stop=True).then_inc(crep, 1)

        def scan_pe(pe, l):
            pe.wait_ge(silu_done, 48 * (l + 1) + 2)
            for piece in range(3):
                pre_pe(pe, l, 0, piece)
            rep_b(pe, l, 0, 0, 0)
            rep_c(pe, l, 0, 0, 0)
            rep_b(pe, l, 0, 1, 0)
            with pe.Fori(0, 2) as bp:
                for si in range(6):
                    s, q = 6 * bp + si, si % 2
                    S = 12 * l + s
                    for n in range(NS):
                        rep_c(pe, l, s, n + 1, q)
                        rep_b(pe, l, s, n + 2, q)
                        if n in PE_PIECE_AT:
                            pre_pe(pe, l, s + 1, PE_PIECE_AT.index(n))
                        for half in range(2):
                            j = 2 * n + half
                            pe.wait_ge(hc_done, 32 * S + j + 1 + CR_HC)
                            if n == 0:
                                pe.wait_ge(y_out, 2 * S + half - 1 + CR_YOUT)
                            nc.tensor.matmul(bank(half), ident, prod[j % 4], start=(n == 0),
                                             stop=(n == NS - 1)).then_inc(y_acc, 1)
                            if n == SKIP_AT:
                                nc.tensor.matmul(bank(half), diag[:, half, :],
                                                 U[:, ds(s * UW + half * TC, TC)], start=False,
                                                 stop=False)

        def out_pe(pe, l):
            pe.wait_ge(gated, 13 * (l + 1) + 1)
            pe.wait_ge(da_ready, 388 * (l + 1))
            with pe.Fori(0, 2) as bp:
                for c in range(3):
                    pe.wait_ge(z_updated, 6 * l + 3 * bp + c - 2 + 3)
                    for i in range(4):
                        par, half = i // 2, i % 2
                        slot = 6 * bp + 3 * par + c
                        last = nc.tensor.matmul(bank(c), wo(l, half, par),
                                                SG[:, ds(slot * UW + half * TC, TC)],
                                                start=(i == 0), stop=(i == 3))
                    last.then_inc(outp_ready, 1)

        def spread_pe(pe, use):
            pe.wait_ge(wtok_ready, use + 1)
            for g in range(TILES):
                last = nc.tensor.matmul(psum[:, 512 + 128 * g:640 + 128 * g], wtok[:, g, :], ident,
                                        start=True, stop=True, skip_group_check=True)
            last.then_inc(wt_mm, 1)

        def experts0_pe(pe):
            pe.wait_ge(wt_split, 4)
            with pe.Fori(0, 3) as kk:
                for r in range(2):
                    k = 2 * kk + r
                    cols = ds(k * TC, TC)
                    pe.wait_ge(h_e0, k + 1)
                    nc.tensor.matmul(bank(4 + r), b2bd, wtf[:, cols], start=True, stop=False,
                                     skip_group_check=True)

                    def down(u):
                        pe.wait_ge(hs_done, 16 * k + u + 1 + 4)
                        par = u % 2
                        nc.tensor.matmul(psum[64 * par:64 * par + 64,
                                              512 * (4 + r):512 * (4 + r) + TC],
                                         w2s[:, u // 2, :], hsc[u % 4], start=False, stop=u >= 14,
                                         skip_group_check=True).then_inc(e_out, 1)

                    for u in range(16):
                        e, par = u // 2, u % 2
                        pe.wait_ge(gelu_done, 16 * k + u - 1 + 2)
                        nc.tensor.matmul(bank(u % 2), w1z[:, e, par, :], Z[:, cols], start=True,
                                         stop=True).then_inc(h1_ready, 1)
                        pe.wait_ge(hs_done, 16 * k + u - 1 + 4)
                        i = 8 * par + e
                        nc.tensor.matmul(bank(2 + u % 2), sel[:, i:i + 1].broadcast_to([128, 128]),
                                         wtb[:, cols], start=True, stop=True).then_inc(wrep, 1)
                        if u >= 2:
                            down(u - 2)
                    down(14)
                    down(15)

        def experts1_pe(pe):
            pe.wait_ge(wt_split, 8)
            pe.wait_ge(sel2_ready, 1)
            with pe.Fori(0, 3) as kk:
                for r in range(2):
                    k = 2 * kk + r
                    cols = ds(k * TC, TC)
                    pe.wait_ge(h_e1, k + 1)
                    nc.tensor.matmul(bank(6 + r), b3bd, wtf[:, cols], start=True, stop=False)

                    def second(e):
                        pe.wait_ge(a1_done, 6 * k + e + 1 + 2)
                        pe.wait_ge(a2_done, 6 * k + e - 1 + 2)
                        nc.tensor.matmul(bank(2 + e % 2), w123[:, 1, e, :], hid[e % 2], start=True,
                                         stop=True).then_inc(l2_ready, 1)
                        pe.wait_ge(hs1_done, 6 * k + e - 1 + 2)
                        nc.tensor.matmul(bank(4 + e % 2), sel2[:, e, :], wtb[:, cols], start=True,
                                         stop=True).then_inc(wrep1, 1)

                    def third(e):
                        pe.wait_ge(hs1_done, 6 * k + e + 1 + 2)
                        nc.tensor.matmul(bank(6 + r), w123[:, 2, e, :], hsc[2 + e % 2], start=False,
                                         stop=e == E1N - 1).then_inc(e1_out, 1)

                    for e in range(E1N + 2):
                        if e < E1N:
                            pe.wait_ge(a1_done, 6 * k + e - 1 + 2)
                            nc.tensor.matmul(bank(e % 2), w123[:, 0, e, :], Z[:, cols], start=True,
                                             stop=True).then_inc(l1_ready, 1)
                        if 1 <= e <= E1N:
                            second(e - 1)
                        if e >= 2:
                            third(e - 2)

        def filter_pe(pe):
            pe.wait_ge(att_loaded, 32)
            pe.wait_ge(a_step, 20)
            pe.wait_ge(normed, 27)
            nc.tensor.matmul(psum[0:48, 0:8], cs, ab[0:64], start=True, stop=True).then_inc(g_mm, 1)
            nc.tensor.matmul(psum[:, 512:576], abrep, ident[0:64, 0:64], start=True, stop=True,
                             skip_group_check=True)
            nc.tensor.matmul(psum[:, 576:640], pw[0:64, 8:9].broadcast_to([64, 128]),
                             ident[0:64, 0:64], start=True, stop=True,
                             skip_group_check=True).then_inc(p_mm, 1)
            mv = mphi.rearrange("o (d e) -> o e d", e=F)

            def q_group(g):
                if g >= 4:
                    pe.wait_ge(q_even, g - 3)
                    pe.wait_ge(q_odd, g - 3)
                for e in range(8):
                    for q in range(2):
                        at = 512 * (2 + g % 4) + SS * e
                        last = nc.tensor.matmul(psum[64 * q:64 * q + 64, at:at + SS],
                                                mv[:, 8 * g + e, :], ct, start=True, stop=True,
                                                skip_group_check=True)
                last.then_inc(q_mm, 1)

            for g in range(4):
                q_group(g)
            pe.wait_ge(g_ready, 1)
            for e in range(F):
                for q in range(2):
                    last = nc.tensor.matmul(psum[64 * q:64 * q + 64, 3584 + 8 * e:3592 + 8 * e],
                                            mv[:, e, :], gk[:, q, :], start=True, stop=True,
                                            skip_group_check=True)
            last.then_inc(kj_mm, 1)
            for g in range(4, 8):
                q_group(g)
            pe.wait_ge(wv_ready, 1)
            for k in range(9):
                if k >= 2:
                    pe.wait_ge(xt_ready, k - 1)
                for bp in range(2):
                    at = bp * TOK + 128 * k
                    last = nc.tensor.matmul(psum[:, 512 * (k % 2) + 128 * bp:
                                                 512 * (k % 2) + 128 * bp + 128],
                                            Z[:, at:at + 128], ident, start=True, stop=True,
                                            skip_group_check=True)
                last.then_inc(xt_mm, 1)
            pe.wait_ge(q_even, 8)
            pe.wait_ge(q_odd, 8)
            for g in range(4):
                for k in range(9):
                    v = 9 * g + k
                    if g == 0:
                        pe.wait_ge(xt_ready, k + 1)
                    if v >= 2:
                        pe.wait_ge(v_copied, v - 1)
                    n = min(16, NCH - 1 - 16 * k)
                    nc.tensor.matmul(
                        bank(2 + v % 2, 32 * n), xt[:, k, g // 2, :, :].rearrange(
                            "p q d -> p (q d)"), wv[:, 0:n, 32 * (g % 2):32 * (g % 2) + 32],
                        start=True, stop=True).then_inc(v_mm, 1)

            def mix_states(bp):
                for g in range(SS // 2):
                    i = SS // 2 * bp + g
                    pe.wait_ge(state_done, 2 * i + 2)
                    if i >= 2:
                        pe.wait_ge(z_copied, i - 1)
                    for k in range(2):
                        at = 512 * (6 + i % 2) + NCH * k
                        last = nc.tensor.matmul(
                            psum[:, at:at + NCH], QB[:, 2 * g + k, :, :].rearrange(
                                "p q e -> p (q e)"), SH[:, bp, 2 * g + k, :], start=True,
                            stop=True, skip_group_check=True)
                    last.then_inc(z_mm, 1)

            def transpose_mixed(bp):
                pe.wait_ge(z_copied, SS // 2 * (bp + 1))
                for g in range(18):
                    i = 18 * bp + g
                    if i >= 2:
                        pe.wait_ge(zt_copied, i - 1)
                    for k in range(min(4, NCH // 2 - 4 * g)):
                        c = 2 * (4 * g + k)
                        at = 512 * (i % 2) + 128 * k
                        last = nc.tensor.matmul(
                            psum[:, at:at + 128], ZS[:, c:c + 2, :].rearrange("p c s -> p (c s)"),
                            ident, start=True, stop=True, skip_group_check=True)
                    last.then_inc(zt_mm, 1)

            def token_outputs(bp):
                pe.wait_ge(zt_copied, 18 * (bp + 1))
                for g in range(NCH // 2):
                    at = 512 * (2 + 3 * bp) + 16 * g
                    last = nc.tensor.matmul(psum[:, at:at + 16], ZT[:, bp, g, :], apair,
                                            start=True, stop=True, skip_group_check=True)
                last.then_inc(f_out, 1)

            mix_states(0)
            pe.wait_ge(kj_ready, 3)
            pe.wait_ge(lg_ready, 24)
            for i in range(CL):
                if i >= 2:
                    pe.wait_ge(h_att, 2 * (i - 1))
                for m in range(KX // 2):
                    wk = (kf if 2 * m < i else kx if 2 * m == i else km)[:, m, :]
                    for q in range(2):
                        base = CL - 1 + i - 2 * m
                        at = 512 * (4 + i % 2)
                        last = nc.tensor.matmul(
                            psum[64 * q:64 * q + 64, at:at + 2 * NCH], wk,
                            LG[:, q, :, base:base + CL * (NCH - 1) + 1:CL], start=(m == 0),
                            stop=(m == KX // 2 - 1), skip_group_check=True)
                last.then_inc(taps_mm, 1)
            transpose_mixed(0)
            mix_states(1)
            pe.wait_ge(h_att, 16)
            token_outputs(0)
            transpose_mixed(1)
            token_outputs(1)

        @block.tensor
        def _(pe):
            pe.wait_ge(setup_loaded, SETUP)
            for par in range(2):
                for f in range(F):
                    last = nc.tensor.matmul(psum[64 * par:64 * par + 64, f * 8:f * 8 + 8],
                                            wt18[:, f, :], dftm[:, 8 * par:8 * par + 8],
                                            start=(f == 0), stop=True, skip_group_check=True)
            last.then_inc(patch_w_ready, 1)
            pe.wait_ge(patch_w_copied, 1)
            for bp in range(2):
                for par in range(2):
                    pe.wait_ge(xload[2 * bp + par], 16)
                for nh in range(2):
                    for j in range(8):
                        for par in range(2):
                            xv = X[:, 2 * bp + par, :].rearrange("p (n r v) -> p n r v", r=4, v=VARS)
                            n0 = 8 * nh + j // 4
                            last = nc.tensor.matmul(
                                psum[64 * par:64 * par + 64,
                                     512 * (1 + 2 * bp + nh):512 * (2 + 2 * bp + nh)],
                                gt[:, j, :], xv[:, n0:n0 + 8, j % 4, :],
                                start=(j == 0), stop=(j == 7))
                last.then_inc(embedded, 1)
            pe.wait_ge(h_ready, 2)
            norm_pe(pe, 0, 0, center, H, None, None)
            for l in range(LAYERS):
                rms_pe(pe, l)
                scan_pe(pe, l)
                out_pe(pe, l)
            pe.wait_ge(z_updated, 15)
            pe.wait_ge(mats_ready, 1)
            norm_pe(pe, 1, 3, centerw, Z, sqz, meaneps)
            pe.wait_ge(normed, 15)
            norm_pe(pe, 2, 4, center, H, None, None)
            pe.wait_ge(normed, 21)
            pe.wait_ge(e0_loaded, 16)
            for g in range(TILES):
                last = nc.tensor.matmul(psum[:, 16 * g:16 * g + 16], Z[:, 128 * g:128 * g + 128],
                                        wr0, start=True, stop=True, skip_group_check=True)
            last.then_inc(logits, 1)
            spread_pe(pe, 0)
            experts0_pe(pe)
            pe.wait_ge(h_e0, 8)
            norm_pe(pe, 3, 5, center, H, None, None)
            filter_pe(pe)
            pe.wait_ge(h_att, 22)
            norm_pe(pe, 4, 6, center, H, None, None)
            pe.wait_ge(normed, 33)
            pe.wait_ge(e1_loaded, 16)
            for k in range(5):
                n = min(512, PADCOLS - 512 * k)
                if k == 0:
                    pe.wait_ge(var_ready, 42)
                last = nc.tensor.matmul(bank(k, n), rw1, Z[:, 512 * k:512 * k + n], start=True,
                                        stop=True)
                last.then_inc(rh_mm, 1)
            pe.wait_ge(rh_done, 5)
            for g in range(TILES):
                last = nc.tensor.matmul(psum[:, 12 * g:12 * g + 12], rhid[:, 128 * g:128 * g + 128],
                                        rw2, start=True, stop=True, skip_group_check=True)
            last.then_inc(logits, 1)
            spread_pe(pe, 1)
            experts1_pe(pe)

        def root_act(act, g, c, scale, bias):
            act.wait_ge(var_ready, g + c + 1)
            nc.scalar.activation(lnv[c], bank(3 + c), ACT.Ln, bias=col_eps(bias),
                                 scale=scale).then_inc(ln_done, 1)
            act.wait_ge(ln_done, g + c + 1)
            nc.scalar.activation(rstd[c], lnv[c], ACT.Exp, scale=-0.5).then_inc(rstd_ready, 1)

        def col_eps(v):
            return vec[:, V_EPS:V_EPS + 1] if v == EPS else vec[:, V_EPS2:V_EPS2 + 1]

        def norm_act(act, cn, rn, scale, bias):
            with act.Fori(0, 2) as bp:
                for c in range(3):
                    act.wait_ge(centered, 6 * cn + 3 * bp + c + 1)
                    nc.scalar.activation(sq[c], bank(c), ACT.Square).then_inc(squared, 1)
                for c in range(3):
                    root_act(act, 6 * rn + 3 * bp, c, scale, bias)

        def rms_act(act, l):
            use = 1 + l
            with act.Fori(0, 2) as bp:
                g = 6 * use + 3 * bp
                for c in range(3):
                    root_act(act, g, c, 1.0, EPS)
                for c in range(3):
                    for par in range(2):
                        slot = 6 * bp + 3 * par + c
                        for w in range(4):
                            i = 8 * c + 4 * par + w
                            half = w % 2
                            act.wait_ge(proj_ready, 48 * l + 24 * bp + i + 1)
                            dst = (U if w < 2 else SG)[:, ds(slot * UW + half * TC, TC)]
                            if w < 2:
                                nc.scalar.activation(dst, bank(6 + w % 2), ACT.Silu,
                                                     bias=col(l, M_CB + half)).then_inc(silu_done, 1)
                            else:
                                nc.scalar.activation(dst, bank(6 + w % 2),
                                                     ACT.Silu).then_inc(silu_done, 1)
                nc.scalar.preload_act_table_set("natural_log_exp_and_others")

        def pre_act_piece(act, l, slot, q, piece):
            p = 13 * l + slot
            if piece == 0:
                act.wait_ge(pre_mm, 3 * p + 1)
                nc.scalar.activation(ssmf, bank(7), ACT.Identity).then_inc(pre_act, 1)
                nc.scalar.activation(bcs[q], bank(7), ACT.Identity).then_inc(bc_cast, 1)
            elif piece < 3:
                act.wait_ge(pre_mm, 3 * p + piece + 1)
                half = piece - 1
                nc.scalar.activation(xdt[:, half * TC:(half + 1) * TC], bank(7), ACT.Identity,
                                     bias=col(l, M_DTB + half)).then_inc(pre_act, 1)
            elif piece == 3:
                act.wait_ge(pre_dve, PD * p + 5)
                nc.scalar.activation(spl, spl, ACT.Exp).then_inc(sp_exp, 1)
            else:
                act.wait_ge(pre_dve, PD * p + 9)
                nc.scalar.activation(spl, spl, ACT.Ln, bias=1.0).then_inc(sp_ln, 1)

        def decay(act, l, s, j, q):
            S = 12 * l + s
            n, half = j // 2, j % 2
            act.wait_ge(scanned, 32 * S + 2 * l + j - 1 + CR_SCAN)
            nc.scalar.activation(bank(5 + j % 2), dt_[q][:, half * TC:(half + 1) * TC], ACT.Exp,
                                 scale=col(l, M_A + half * NS + n)).then_inc(da_ready, 1)

        def copy_c(act, l, s, n):
            act.wait_ge(crep, 193 * l + 16 * s + n + 1)
            act.wait_ge(hc_done, 32 * (12 * l + s) + 2 * n - 2 + CR_HC)
            nc.scalar.activation(csb[n % 2], bank(4), ACT.Identity).then_inc(ccopied, 1)

        def scan_act(act, l):
            for piece in range(5):
                pre_act_piece(act, l, 0, 0, piece)
            act.wait_ge(pre_dve, PD * 13 * l + 11)
            for j in range(4):
                decay(act, l, 0, j, 0)
                if j == 1:
                    copy_c(act, l, 0, 0)
            with act.Fori(0, 2) as bp:
                for si in range(6):
                    s, q = 6 * bp + si, si % 2
                    S = 12 * l + s
                    for n in range(1, NS):
                        if n > 1:
                            decay(act, l, s, 2 * n, q)
                        copy_c(act, l, s, n)
                        if n > 1:
                            decay(act, l, s, 2 * n + 1, q)
                        if n in ACT_PIECE_AT:
                            pre_act_piece(act, l, s + 1, 1 - q, ACT_PIECE_AT.index(n))
                    act.wait_ge(pre_dve, PD * (13 * l + s + 1) + 11)
                    for j in range(2):
                        decay(act, l, s + 1, j, 1 - q)
                    copy_c(act, l, s + 1, 0)
                    for half in range(2):
                        act.wait_ge(y_acc, 32 * S + 31 + half + CR_YACC)
                        act.wait_ge(gated, 13 * l + s + 2)
                        nc.scalar.activation(y1[:, half * TC:(half + 1) * TC], bank(half),
                                             ACT.Identity).then_inc(y_out, 1)
                        decay(act, l, s + 1, 2 + half, 1 - q)

        def top2_act(act, use):
            act.wait_ge(r_step, t["r_top"][use])
            d = rt[:, T_SMALL + 36 * 4:T_SMALL + 36 * 5]
            nc.scalar.activation(d, d, ACT.Exp).then_inc(r_exp, 1)

        def spread_act(act, use):
            act.wait_ge(wt_mm, use + 1)
            nc.scalar.activation(wtf, psum[:, 512:512 + PADCOLS], ACT.Identity).then_inc(
                wt_copied, 1)
            nc.scalar.activation(wtb, psum[:, 512:512 + PADCOLS], ACT.Identity).then_inc(wt_cast, 1)

        def filter_act(act):
            act.wait_ge(qb_zero, 1)

            def q_even_group(g):
                act.wait_ge(q_mm, g + 1)
                nc.scalar.activation(QB[0:64, :, 0, 8 * g:8 * g + 8], psum[
                    0:64, 512 * (2 + g % 4):512 * (3 + g % 4)].rearrange("p (e s) -> p s e", e=8),
                    ACT.Identity).then_inc(q_even, 1)

            for g in range(8):
                q_even_group(g)
            for k in range(9):
                act.wait_ge(xt_mm, k + 1)
                nc.scalar.activation(xt[:, k, :, :, :], psum[:, 512 * (k % 2):512 * (k % 2) + 256]
                                     .rearrange("p (b q d) -> p b q d", b=2, q=2),
                                     ACT.Identity).then_inc(xt_ready, 1)
            for v in range(36):
                g, k = v // 9, v % 9
                n = min(16, NCH - 1 - 16 * k)
                act.wait_ge(v_mm, v + 1)
                nc.scalar.activation(
                    SH[:, g // 2, 32 * (g % 2):32 * (g % 2) + 32, 16 * k + 1:16 * k + 1 + n],
                    bank(2 + v % 2, 32 * n).rearrange("p (c s) -> p s c", s=32),
                    ACT.Identity).then_inc(v_copied, 1)
            for i in range(SS):
                g = i % (SS // 2)
                act.wait_ge(z_mm, i + 1)
                if i == SS // 2:
                    act.wait_ge(zt_mm, 18)
                nc.scalar.activation(
                    ZS[:, :, 2 * g:2 * g + 2], bank(6 + i % 2, 2 * NCH).rearrange(
                        "p (k c) -> p c k", k=2), ACT.Identity).then_inc(z_copied, 1)

        @block.scalar
        def _(act):
            act.wait_ge(setup_loaded, SETUP)
            for l in range(LAYERS):
                a_cols = mw[l][:, W_C + M_A:W_C + MCOLS]
                nc.scalar.activation(a_cols, a_cols, ACT.Exp).then_inc(a_exp, 1)
            for bp in range(2):
                act.wait_ge(embedded, bp + 1)
                for nh in range(2):
                    dst = H[:, bp * TOK:bp * TOK + VARS * NPATCH].rearrange(
                        "p (v n) -> p n v", v=VARS)[:, 8 * nh:8 * nh + 8, :]
                    last = nc.scalar.activation(
                        dst, psum[:, 512 * (1 + 2 * bp + nh):512 * (2 + 2 * bp + nh)].rearrange(
                            "p (n v) -> p n v", v=VARS), ACT.Identity)
                last.then_inc(h_ready, 1)
            nc.scalar.preload_act_table_set("natural_log_exp_and_others")
            norm_act(act, 0, 0, 1.0 + EPS, EPS * EPS)
            for l in range(LAYERS):
                rms_act(act, l)
                scan_act(act, l)
            norm_act(act, 1, 3, 1.0, EPS * EPS)
            norm_act(act, 2, 4, 1.0 + EPS, EPS * EPS)
            top2_act(act, 0)
            spread_act(act, 0)
            with act.Fori(0, 3) as kk:
                for r in range(2):
                    k = 2 * kk + r
                    for u in range(16):
                        act.wait_ge(h1_ready, 16 * k + u + 1)
                        act.wait_ge(hs_done, 16 * k + u - 3 + 4)
                        nc.scalar.activation(hid[u % 4], bank(u % 2), ACT.Gelu,
                                             bias=b1c[:, u // 2:u // 2 + 1]).then_inc(gelu_done, 1)
            nc.scalar.preload_act_table_set("natural_log_exp_and_others")
            norm_act(act, 3, 5, 1.0, EPS)
            filter_act(act)
            norm_act(act, 4, 6, 1.0, EPS)
            for k in range(5):
                n = min(512, PADCOLS - 512 * k)
                act.wait_ge(rh_mm, k + 1)
                nc.scalar.activation(rhid[:, 512 * k:512 * k + n], bank(k, n), ACT.Relu,
                                     bias=rb1).then_inc(rh_done, 1)
            act.wait_ge(r_step, t["r_soft"])
            nc.scalar.activation(rt[:, 0:36 * E1N], rt[:, 0:36 * E1N], ACT.Exp).then_inc(r_exp, 1)
            top2_act(act, 1)
            spread_act(act, 1)
            with act.Fori(0, 3) as kk:
                for r in range(2):
                    k = 2 * kk + r
                    for e in range(E1N + 1):
                        if e < E1N:
                            act.wait_ge(l1_ready, 6 * k + e + 1)
                            act.wait_ge(l2_ready, 6 * k + e - 1 + 2)
                            nc.scalar.activation(hid[e % 2], bank(e % 2), ACT.Relu,
                                                 bias=eb12[:, e:e + 1]).then_inc(a1_done, 1)
                        if e >= 1:
                            f = e - 1
                            act.wait_ge(l2_ready, 6 * k + f + 1 + 2)
                            act.wait_ge(hs1_done, 6 * k + f - 1 + 2)
                            nc.scalar.activation(hid[2 + f % 2], bank(2 + f % 2), ACT.Relu,
                                                 bias=eb12[:, 6 + f:7 + f]).then_inc(a2_done, 1)

        def norm_dve(dve, cn, rn, kind):
            with dve.Fori(0, 2) as bp:
                g = 6 * rn + 3 * bp
                if kind == "final":
                    for c in range(3):
                        z = Z[:, ds(bp * TOK + c * TC, TC)]
                        dve.wait_ge(var_ready, g)
                        nc.vector.tensor_tensor(sqz[c], z, z, ALU.mult).then_inc(zsq, 1)
                for c in range(3):
                    dve.wait_ge(rstd_ready, g + c + 1)
                    cols = ds(bp * TOK + c * TC, TC)
                    if kind in ("plain", "lags"):
                        if kind == "lags":
                            dve.wait_ge(lg_zero, 1)
                            for q in range(2):
                                for tap in range(2):
                                    rows = slice(64 * q, 64 * q + 64)
                                    at = q * 2 * AW + bp * AW + CL - 1 + tap + c * TC
                                    nc.vector.tensor_tensor(
                                        hn2[64 * tap:64 * tap + 64, ds(at, TC)], bank(c)[rows],
                                        rstd[c][rows], ALU.mult).then_inc(lg_ready, 1)
                        nc.vector.tensor_tensor(Z[:, cols], bank(c), rstd[c],
                                                ALU.mult).then_inc(normed, 1)
                        continue
                    nc.vector.tensor_tensor(lnv[c], bank(c), rstd[c], ALU.mult).then_inc(scaled, 1)
                    dve.wait_ge(scaled, 6 * cn + 3 * bp + c + 1)
                    if kind == "gain":
                        nc.vector.tensor_scalar(Z[:, cols], lnv[c], vec[:, V_G0:V_G0 + 1],
                                                vec[:, V_B0:V_B0 + 1], ALU.mult,
                                                ALU.add).then_inc(normed, 1)
                    elif kind == "pre":
                        nc.vector.tensor_scalar(Z[:, cols], lnv[c], vec[:, V_PREG:V_PREG + 1],
                                                vec[:, V_PREB:V_PREB + 1], ALU.mult,
                                                ALU.add).then_inc(normed, 1)
                    elif kind == "final":
                        nc.vector.tensor_scalar(lnv[c], lnv[c], vec[:, V_POSTG:V_POSTG + 1],
                                                vec[:, V_POSTB:V_POSTB + 1], ALU.mult,
                                                ALU.add).then_inc(shifted, 1)
                        dve.wait_ge(shifted, 3 * bp + c + 1)
                        nc.vector.tensor_tensor(H[:, cols], H[:, cols], lnv[c],
                                                ALU.add).then_inc(normed, 1)

        def rms_dve(dve, l, then):
            use = 1 + l
            if l == 0:
                dve.wait_ge(normed, 6 + 3)
                dve.wait_ge(embedded, 2)
                then(nc.vector.memset(U[:, SLOTS * UW:], 0.0))
            else:
                dve.wait_ge(z_updated, 6 * l + 3)
            for half in range(2):
                then(nc.vector.tensor_scalar(diag[:, half, :], ident,
                                             col(l, M_D + half), None, ALU.mult))
            with dve.Fori(0, 2) as bp:
                g = 6 * use + 3 * bp
                for c in range(3):
                    z = Z[:, ds(bp * TOK + c * TC, TC)]
                    dve.wait_ge(var_ready, g)
                    nc.vector.tensor_tensor(sq[c], z, z, ALU.mult).then_inc(squared, 1)
                for c in range(3):
                    dve.wait_ge(rstd_ready, g + c + 1)
                    for par in range(2):
                        slot = 6 * bp + 3 * par + c
                        rows = slice(64 * par, 64 * par + 64)
                        at = 32 * l + 16 * bp + (0, 4, 10)[c] + (2, 3, 3)[c] * par
                        if c > 0:
                            dve.wait_ge(tap_step, at)
                            nc.vector.tensor_copy(
                                hn2[:, ds(slot * SW + 1, 3)],
                                hn2[:, ds((slot - 1) * SW + TC + 1, 3)]).then_inc(tap_step, 1)
                            dve.wait_ge(tap_step, at + 1)
                        for tap in range(2):
                            nc.vector.tensor_tensor(
                                hn2[64 * tap:64 * tap + 64, ds(slot * SW + 3 + tap, TC)],
                                Z[rows, ds(bp * TOK + c * TC, TC)], rstd[c][rows],
                                ALU.mult).then_inc(tap_step, 1)

        def pre_dve_piece(dve, l, slot, q, piece):
            p = 13 * l + slot
            b = bcs[q]
            lo, hi = slice(64, 128), slice(96, 128)
            if piece == 0:
                dve.wait_ge(bc_cast, p + 1)
                dve.wait_ge(pre_act, 3 * p + 2)
                nc.vector.tensor_tensor(res[lo], ssmf[lo], b[lo], ALU.subtract).then_inc(pre_dve, 1)
                dve.wait_ge(pre_dve, PD * p + 1)
                nc.vector.tensor_copy(b[lo], res[lo]).then_inc(pre_dve, 1)
                dve.wait_ge(pre_dve, PD * p + 2)
                nc.vector.tensor_tensor(res[hi], res[hi], b[hi], ALU.subtract).then_inc(pre_dve, 1)
                dve.wait_ge(pre_dve, PD * p + 3)
                nc.vector.tensor_copy(b[hi], res[hi]).then_inc(pre_dve, 1)
            elif piece == 1:
                dve.wait_ge(pre_act, 3 * p + 4)
                nc.vector.tensor_scalar(spl, xdt, 40.0, None, ALU.min).then_inc(pre_dve, 1)
            elif piece == 2:
                dve.wait_ge(sp_exp, p + 1)
                tmp = dtu[q]
                nc.vector.tensor_scalar(tmp, spl, 1.0 / 3.0, -0.5, ALU.mult,
                                        ALU.add).then_inc(pre_dve, 1)
                dve.wait_ge(pre_dve, PD * p + 6)
                nc.vector.tensor_tensor(tmp, tmp, spl, ALU.mult).then_inc(pre_dve, 1)
                dve.wait_ge(pre_dve, PD * p + 7)
                nc.vector.scalar_tensor_tensor(dt_[q], tmp, 1.0, spl, ALU.add,
                                               ALU.mult).then_inc(pre_dve, 1)
                dve.wait_ge(pre_dve, PD * p + 8)
                nc.vector.tensor_scalar(tmp, spl, SERIES_BELOW, None, ALU.is_ge).then_inc(pre_dve, 1)
            elif piece == 3:
                dve.wait_ge(sp_ln, p + 1)
                nc.vector.tensor_tensor(spl, spl, xdt, ALU.max).then_inc(pre_dve, 1)
            elif piece == 4:
                nc.vector.copy_predicated(dt_[q], dtu[q].bitcast(mybir.dt.int32),
                                          spl).then_inc(pre_dve, 1)
            else:
                dve.wait_ge(pre_dve, PD * p + 11)
                nc.vector.tensor_tensor(dtu[q], dt_[q], U[:, ds(slot * UW, UW)],
                                        ALU.mult).then_inc(pre_dve, 1)

        def drive(dve, l, s, j, q):
            S = 12 * l + s
            n, half = j // 2, j % 2
            dve.wait_ge(brep, 194 * l + 16 * s + n + 1)
            dve.wait_ge(scanned, 32 * S + 2 * l + j - 3 + CR_SCAN)
            if j == 0:
                dve.wait_ge(pre_dve, PD * (13 * l + s) + 12)
            nc.vector.tensor_tensor(dbu[j % 4],
                                    dtu[q][:, half * TC:(half + 1) * TC], bank(2 + n % 2),
                                    ALU.mult).then_inc(dbu_done, 1)

        def scan_dve(dve, l):
            dve.wait_ge(silu_done, 48 * (l + 1) + 2)
            for piece in range(6):
                if piece == 4:
                    dve.wait_ge(pre_dve, PD * 13 * l + 10)
                    nc.vector.memset(ringc[:, 31:32], 0.0).then_inc(spare, 1)
                pre_dve_piece(dve, l, 0, 0, piece)
            with dve.Fori(0, 2) as bp:
                for si in range(6):
                    s, q, first = 6 * bp + si, si % 2, si % 3 == 0
                    S = 12 * l + s
                    drive(dve, l, s, 0, q)
                    for j in range(2 * NS):
                        if j == DVE_PIECE_AT[4]:
                            dve.wait_ge(pre_dve, PD * (13 * l + s + 1) + 10)
                        if j + 1 < 2 * NS:
                            drive(dve, l, s, j + 1, q)
                        dve.wait_ge(da_ready, 388 * l + 32 * s + j + 1)
                        dve.wait_ge(dbu_done, 32 * S + j + 1 + CR_DBU)
                        nc.vector.tensor_tensor_scan(
                            HB[:, j, :], bank(5 + j % 2), dbu[j % 4],
                            0.0 if first else HB[:, j, TC - 1:TC], ALU.mult,
                            ALU.add).then_inc(scanned, 1)
                        if j in DVE_PIECE_AT:
                            pre_dve_piece(dve, l, s + 1, 1 - q, DVE_PIECE_AT.index(j))
            dve.wait_ge(da_ready, 388 * l + 386)
            nc.vector.memset(ringc[:, 30:31], 0.0).then_inc(scanned, 2)

        def out_dve(dve, l):
            with dve.Fori(0, 2) as bp:
                for c in range(3):
                    dve.wait_ge(outp_ready, 6 * l + 3 * bp + c + 1)
                    z = Z[:, ds(bp * TOK + c * TC, TC)]
                    nc.vector.tensor_tensor(z, z, bank(c), ALU.add).then_inc(z_updated, 1)

        r_count = [0]

        def route_dve(dve, use, n, br, idx):
            G = 2 * TILES

            def then(ins):
                r_count[0] += 1
                ins.then_inc(r_step, 1)
                dve.wait_ge(r_step, r_count[0])

            def wide(i):
                return rt[:, 288 * i:288 * i + G * n].rearrange("p (g e) -> p g e", e=n)

            def small(i):
                return rt[:, T_SMALL + 36 * i:T_SMALL + 36 * i + 36]

            def spread(v):
                return v.unsqueeze(2).broadcast_to([128, G, n])

            S, eq, oh1, S2, oh2 = (wide(i) for i in range(5))
            row = lambda v: v.unsqueeze(1).broadcast_to([128, G, n])
            then(nc.vector.tensor_tensor(S, psum[:, 0:G * n].rearrange("p (g e) -> p g e", e=n),
                                         row(br), ALU.add))
            if use == 1:
                then(nc.vector.tensor_reduce(small(0), S, AX.X, ALU.max))
                then(nc.vector.tensor_tensor(S, S, spread(small(0)), ALU.subtract))
                assert r_count[0] == t["r_soft"], r_count[0]
                dve.wait_ge(r_exp, 2)
                then(nc.vector.tensor_reduce(small(1), S, AX.X, ALU.add))
                then(nc.vector.reciprocal(small(1), small(1)))
                then(nc.vector.tensor_tensor(S, S, spread(small(1)), ALU.mult))

            def first(src, m, oh):
                then(nc.vector.tensor_reduce(small(m), src, AX.X, ALU.max))
                then(nc.vector.tensor_tensor(eq, src, spread(small(m)), ALU.is_equal))
                then(nc.vector.tensor_tensor(eq, eq, row(idx), ALU.mult))
                then(nc.vector.tensor_reduce(small(3), eq, AX.X, ALU.max))
                then(nc.vector.tensor_tensor(oh, eq, spread(small(3)), ALU.is_equal))

            first(S, 0, oh1)
            then(nc.vector.tensor_scalar(S2, oh1, -BIG, None, ALU.mult))
            then(nc.vector.tensor_tensor(S2, S2, S, ALU.add))
            first(S2, 1, oh2)
            then(nc.vector.tensor_tensor(small(4), small(1), small(0), ALU.subtract))
            assert r_count[0] == t["r_top"][use], r_count[0]
            dve.wait_ge(r_exp, 1 + 2 * use)
            then(nc.vector.tensor_scalar(small(5), small(4), 1.0, None, ALU.add))
            then(nc.vector.reciprocal(small(5), small(5)))
            then(nc.vector.tensor_tensor(small(6), small(4), small(5), ALU.mult))
            then(nc.vector.tensor_tensor(oh1, oh1, spread(small(5)), ALU.mult))
            then(nc.vector.tensor_tensor(oh2, oh2, spread(small(6)), ALU.mult))
            then(nc.vector.tensor_tensor(oh1, oh1, oh2, ALU.add))
            dve.wait_ge(wtok_zero, use + 1)
            for part in (0, 64, 96):
                last = nc.vector.tensor_copy(wtok[:, :, part:part + 2 * n],
                                             oh1.rearrange("p (g q) e -> p g (q e)", q=2))
            last.then_inc(wtok_ready, 1)
            lo, hi = slice(64, 128), slice(96, 128)
            dve.wait_ge(wt_cast, use + 1)
            nc.vector.tensor_tensor(wres[lo], wtf[lo], wtb[lo], ALU.subtract).then_inc(wt_split, 1)
            dve.wait_ge(wt_split, 4 * use + 1)
            nc.vector.tensor_copy(wtb[lo], wres[lo]).then_inc(wt_split, 1)
            dve.wait_ge(wt_split, 4 * use + 2)
            nc.vector.tensor_tensor(wres[hi], wres[hi], wtb[hi], ALU.subtract).then_inc(wt_split, 1)
            dve.wait_ge(wt_split, 4 * use + 3)
            nc.vector.tensor_copy(wtb[hi], wres[hi]).then_inc(wt_split, 1)

        def filter_dve_weights(dve):
            n = [0]

            def then(ins):
                n[0] += 1
                ins.then_inc(a_step, 1)
                dve.wait_ge(a_step, n[0])

            dve.wait_ge(att_loaded, 32)
            nc.vector.memset(pw[:, 0:1], 1.0)
            nc.vector.tensor_copy(pw[:, 1:2], acol)
            nc.vector.tensor_copy(ab[:, 0:1], bcol)
            then(nc.vector.tensor_copy(abr[:, 7:8], bcol))
            for j in range(1, 8):
                then(nc.vector.tensor_tensor(pw[:, j + 1:j + 2], pw[:, j:j + 1], acol, ALU.mult))
            for j in range(1, 8):
                nc.vector.tensor_tensor(abr[:, 7 - j:8 - j], pw[:, j:j + 1], bcol, ALU.mult)
                then(nc.vector.tensor_tensor(ab[:, j:j + 1], pw[:, j:j + 1], bcol, ALU.mult))
            then(nc.vector.tensor_copy(abrep.rearrange("p (c i) -> p c i", c=16),
                                       abr[0:64].unsqueeze(1).broadcast_to([64, 16, 8])))
            then(nc.vector.memset(gfull, 0.0))
            then(nc.vector.memset(apair, 0.0))
            then(nc.vector.tensor_copy(apair[0:64, 0:8], pw[0:64, 1:9]))
            then(nc.vector.tensor_copy(apair[64:128, 8:16], pw[64:128, 1:9]))

        def filter_dve(dve):
            dve.wait_ge(g_mm, 1)
            nc.vector.tensor_tensor(gfull, psum[0:48, 0:8], m2, ALU.add).then_inc(a_step, 1)
            dve.wait_ge(a_step, 21)
            for q in range(2):
                nc.vector.tensor_copy(gk[:, q, 0:4], gfull[:, q:q + 7:2])
                last = nc.vector.tensor_copy(gk[:, q, 4:8], m2[:, q:q + 7:2])
            last.then_inc(g_ready, 1)
            dve.wait_ge(p_mm, 1)
            nc.vector.tensor_copy(a8row, psum[:, 576:640]).then_inc(a_step, 1)
            nc.vector.tensor_tensor(
                wv, psum[:, 512:576].unsqueeze(1).broadcast_to([128, 16, 64]),
                cmask.unsqueeze(2).broadcast_to([128, 16, 64]), ALU.mult).then_inc(wv_ready, 1)
            dve.wait_ge(qb_zero, 1)
            for g in range(8):
                dve.wait_ge(q_mm, g + 1)
                nc.vector.tensor_copy(QB[64:128, :, 1, 8 * g:8 * g + 8], psum[
                    64:128, 512 * (2 + g % 4):512 * (3 + g % 4)].rearrange(
                        "p (e s) -> p s e", e=8)).then_inc(q_odd, 1)
                if g == 3:
                    dve.wait_ge(kj_mm, 1)
                    kp = psum[:, 3584:4096].rearrange("p (e f m) -> p f m e", e=F, f=2)
                    nc.vector.tensor_copy(kf, kp[:, 0, :, :]).then_inc(kj_ready, 1)
                    nc.vector.tensor_copy(km, kp[:, 1, :, :]).then_inc(kj_ready, 1)
                    nc.vector.tensor_copy(kx[0:64], kp[0:64, 0, :, :])
                    nc.vector.tensor_copy(kx[64:128], kp[64:128, 1, :, :]).then_inc(kj_ready, 1)
            for bp in range(2):
                nc.vector.memset(SH[:, bp, :, 0:1], 0.0).then_inc(a_step, 1)
            dve.wait_ge(a_step, 24)
            for g in range(4):
                dve.wait_ge(v_copied, 9 * (g + 1))
                for i in range(32):
                    n = 32 * (g % 2) + i
                    line = SH[:, g // 2, n, :]
                    nc.vector.tensor_tensor_scan(
                        line, a8row[:, n:n + 1].broadcast_to([128, NCH]), line, 0.0, ALU.mult,
                        ALU.add).then_inc(state_done, 1)
            for i in range(CL):
                n = NCH if i < TOK - CL * (NCH - 1) else NCH - 1
                dve.wait_ge(taps_mm, i + 1)
                for bp in range(2):
                    at = bp * TOK + i
                    h = H[:, at:at + CL * (n - 1) + 1:CL]
                    nc.vector.tensor_tensor(h, h, psum[:, 512 * (4 + i % 2) + NCH * bp:
                                                       512 * (4 + i % 2) + NCH * bp + n],
                                            ALU.add).then_inc(h_att, 1)
            for bp in range(2):
                for g in range(18):
                    i, n = 18 * bp + g, min(4, NCH // 2 - 4 * g)
                    dve.wait_ge(zt_mm, i + 1)
                    nc.vector.tensor_copy(ZT[:, bp, 4 * g:4 * g + n, :], bank(
                        i % 2, 128 * n).rearrange("p (k m) -> p k m", m=128)).then_inc(zt_copied, 1)
                dve.wait_ge(f_out, bp + 1)
                dve.wait_ge(h_att, 16)
                for c in range(3):
                    n = min(512, TOK - 512 * c)
                    h = H[:, bp * TOK + 512 * c:bp * TOK + 512 * c + n]
                    nc.vector.tensor_tensor(h, h, bank(2 + 3 * bp + c, n),
                                            ALU.add).then_inc(h_att, 1)

        @block.vector
        def _(dve):
            steps = [0]

            def then(ins):
                steps[0] += 1
                ins.then_inc(dve_step, 1)
                dve.wait_ge(dve_step, steps[0])

            for i, (ring, count) in enumerate(((scanned, CR_SCAN), (dbu_done, CR_DBU),
                                               (hc_done, CR_HC), (y_acc, CR_YACC),
                                               (ccopied, CR_CC), (y_out, CR_YOUT), (normed, 3),
                                               (silu_done, 2), (z_updated, 3), (pre_act, 1),
                                               (gated, 1), (gelu_done, 2), (hs_done, 4),
                                               (e_out, 4), (h_e0, 2), (a1_done, 2), (a2_done, 2),
                                               (l2_ready, 2), (hs1_done, 2), (e1_out, 2),
                                               (h_e1, 2))):
                nc.vector.memset(ringc[:, i:i + 1], 0.0).then_inc(ring, count)
            dve.wait_ge(setup_loaded, SETUP)
            dve.wait_ge(zeroed, 2)
            dve.wait_ge(patch_w_ready, 1)
            nc.vector.tensor_copy(gt, psum[:, 0:512].rearrange("p (f j) -> p j f", j=8)).then_inc(
                patch_w_copied, 1)
            then(nc.vector.tensor_copy(sel[:, :], selc))
            for l in range(LAYERS):
                for k in range(2):
                    then(nc.vector.tensor_tensor(wu(l)[:, k, :], inp[l][:, 0:D], cwt[l][:, k, :],
                                                 ALU.mult))
                then(nc.vector.tensor_scalar(mw[l][:, W_U:W_U + 512], mw[l][:, W_U:W_U + 512],
                                             col(l, M_NW), None, ALU.mult))
                then(nc.vector.tensor_scalar(mw[l][0:64, W_G:W_G + D], inp[l][0:64, D:2 * D],
                                             col(l, M_NW)[0:64], None, ALU.mult))
            for l in range(LAYERS):
                dve.wait_ge(a_exp, l + 1)
                then(nc.vector.tensor_scalar(mw[l][:, W_C + M_A:W_C + MCOLS],
                                             mw[l][:, W_C + M_A:W_C + MCOLS], -1.0, None, ALU.mult))
            norm_dve(dve, 0, 0, "pre")
            for l in range(LAYERS):
                rms_dve(dve, l, then)
                scan_dve(dve, l)
                out_dve(dve, l)
            then(nc.vector.tensor_scalar(centerw, center, vec[:, V_NFW:V_NFW + 1], None,
                                         ALU.mult))
            nc.vector.tensor_scalar(meaneps, mean, EPS, None, ALU.mult).then_inc(mats_ready, 1)
            norm_dve(dve, 1, 3, "final")
            norm_dve(dve, 2, 4, "gain")
            dve.wait_ge(e0_loaded, 16)
            dve.wait_ge(logits, 1)
            route_dve(dve, 0, E0, br0, idx0)
            with dve.Fori(0, 3) as kk:
                for r in range(2):
                    k = 2 * kk + r
                    for u in range(16):
                        dve.wait_ge(gelu_done, 16 * k + u + 1 + 2)
                        dve.wait_ge(wrep, 16 * k + u + 1)
                        dve.wait_ge(e_out, 16 * k + u - 3 + 4)
                        nc.vector.tensor_tensor(hsc[u % 4], hid[u % 4], bank(2 + u % 2),
                                                ALU.mult).then_inc(hs_done, 1)
                    dve.wait_ge(e_out, 16 * k + 16 + 4)
                    h = H[:, ds(k * TC, TC)]
                    nc.vector.tensor_tensor(h, h, bank(4 + r), ALU.add).then_inc(h_e0, 1)
            filter_dve_weights(dve)
            norm_dve(dve, 3, 5, "lags")
            filter_dve(dve)
            norm_dve(dve, 4, 6, "plain")
            dve.wait_ge(e1_loaded, 16)
            nc.vector.tensor_copy(sel2, sel2f.rearrange("p (e m) -> p e m", e=E1N)).then_inc(
                sel2_ready, 1)
            dve.wait_ge(logits, 2)
            route_dve(dve, 1, E1N, br1, idx1)
            with dve.Fori(0, 3) as kk:
                for r in range(2):
                    k = 2 * kk + r
                    for e in range(E1N):
                        dve.wait_ge(a2_done, 6 * k + e + 1 + 2)
                        dve.wait_ge(wrep1, 6 * k + e + 1)
                        dve.wait_ge(e1_out, 6 * k + e - 1 + 2)
                        nc.vector.tensor_tensor(hsc[2 + e % 2], hid[2 + e % 2], bank(4 + e % 2),
                                                ALU.mult).then_inc(hs1_done, 1)
                    dve.wait_ge(e1_out, 6 * k + 6 + 2)
                    h = H[:, ds(k * TC, TC)]
                    nc.vector.tensor_tensor(h, h, bank(6 + r), ALU.add).then_inc(h_e1, 1)


def _layout(i):
    a = {k: np.asarray(v) for k, v in i.items()}
    f4 = np.float32
    dup = lambda v: np.concatenate([v, v], axis=0)
    d = {}
    x = a["x"].reshape(BATCH, CH, TIME // 2, 2, VARS).transpose(3, 1, 0, 2, 4)
    edge = np.repeat(x[1:2, :, :, -1:, :], STRIDE // 2, axis=3)
    edge = np.concatenate([edge, edge], axis=0)
    d["x"] = np.concatenate([x, edge], axis=3).reshape(128, BATCH * XW)
    w18 = np.zeros((18, 4096 + PATCH), f4)
    w18[:, :4096] = a["L0_tok_W"].reshape(F, 2, FREQ, CH).transpose(1, 2, 0, 3).reshape(18, 4096)
    ang = 2 * np.pi * np.outer(np.arange(FREQ), np.arange(PATCH)) / PATCH
    dft = np.concatenate([np.cos(ang), -np.sin(ang)]) / np.sqrt(PATCH)
    w18[:, 4096:] = dft.reshape(18, 8, 2).transpose(0, 2, 1).reshape(18, PATCH)
    d["w18"] = w18
    cst = np.zeros((128, C_SIZE), f4)
    eye = np.eye(128)
    blk = np.kron(np.eye(2), np.full((F, F), 1.0 / F))
    cst[:, 0:128], cst[:, 128:256], cst[:, 256:384] = eye, eye - blk, blk
    for part in (0, 64, 96):
        cst[part:part + 32, 384:416] = np.eye(32)
    for v, n in ((V_PREG, "L0_attn_pre_g"), (V_PREB, "L0_attn_pre_b"), (V_POSTG, "L0_attn_post_g"),
                 (V_POSTB, "L0_attn_post_b"), (V_NFW, "L0_attn_normf_w"), (V_G0, "L0_ffn_gamma"),
                 (V_B0, "L0_ffn_beta")):
        cst[:, 416 + v] = dup(a[n])
    cst[:, 416 + V_EPS], cst[:, 416 + V_EPS2] = EPS, EPS * EPS
    d["cst"] = cst
    d["txt"] = a["txt"].reshape(2, 2, TXT, F).transpose(1, 3, 0, 2).reshape(128, 2 * TXT)
    inp = np.zeros((128, 2048), f4)
    for l in range(LAYERS):
        inp[:, 1024 * l:1024 * l + 512] = dup(a["L0_attn_inproj_w"][l].T)
        cw = a["L0_attn_conv_w"][l, :, 0, :].T
        for tap in range(2):
            for k in range(2):
                inp[64 * tap:64 * tap + 64, 1024 * l + 512 + 256 * k:1024 * l + 768 + 256 * k] = \
                    cw[KC - 1 - (2 * k + tap)]
        m = np.zeros((128, W_SIZE), f4)
        xp = a["L0_attn_xproj_w"][l].T.reshape(2, 128, R + 2 * NS)
        for h in range(2):
            at = W_X + 128 * h
            for part in (0, 64, 96):
                m[:, at + part:at + part + 32] = xp[h][:, R:]
            m[:, at + 32:at + 48] = xp[h][:, :R]
            m[:, W_O + 192 * h + 64:W_O + 192 * h + 128] = \
                a["L0_attn_outproj_w"][l].T[128 * h:128 * h + 128]
            for c, n in ((M_CB, "conv_b"), (M_DTB, "dtproj_b"), (M_D, "D_param")):
                m[:, W_C + c + h] = a["L0_attn_" + n][l][128 * h:128 * h + 128]
            m[:, W_C + M_A + NS * h:W_C + M_A + NS * (h + 1)] = \
                a["L0_attn_A_log"][l][128 * h:128 * h + 128]
        m[32:48, W_DT:W_DT + D] = a["L0_attn_dtproj_w"][l].T
        m[:, W_C + M_NW] = dup(a["L0_attn_norm_w"][l])
        d[f"mw{l}"] = m
    d["inp"] = inp
    e0 = np.zeros((128, E0_SIZE), f4)
    w1 = e0[:, 0:2048].reshape(128, E0, 2, HID0)
    for q in range(2):
        rows = slice(64 * q, 64 * q + 64)
        w1[rows, :, q, :] = a["L0_ffn_W1"].transpose(1, 0, 2)
        e0[rows, 2560 + 8 * q:2568 + 8 * q] = a["L0_ffn_Wr"]
        e0[8 * q:8 * q + 8, 2600 + 64 * q:2664 + 64 * q] = a["L0_ffn_b2"]
    e0[:, 0:2048] = w1.reshape(128, 2048)
    e0[:, 2048:2560] = a["L0_ffn_W2"].transpose(1, 0, 2).reshape(HID0, E0 * F)
    e0[:, 2576:2584] = a["L0_ffn_b1"].T
    e0[:, 2584:2592] = a["L0_ffn_br"]
    e0[:, 2592:2600] = np.arange(E0, 0, -1)
    d["e0"] = e0
    e1 = np.zeros((128, E1_SIZE), f4)
    wb = np.zeros((128, 3, E1N, 128), f4)
    sel2 = np.zeros((128, E1N, 128), f4)
    for q in range(2):
        rows = slice(64 * q, 64 * q + 64)
        for k in range(3):
            wb[rows, k, :, rows] = a[f"L1_ffn_expert_w{k + 1}"].transpose(1, 0, 2)
        e1[rows, 2304 + RH * q:2304 + RH * (q + 1)] = a["L1_ffn_router_w1"]
        e1[RH * q:RH * (q + 1), 2432 + E1N * q:2432 + E1N * (q + 1)] = a["L1_ffn_router_w2"]
        e1[RH * q:RH * (q + 1), 2456] = a["L1_ffn_router_b1"]
        e1[rows, 2457:2463] = a["L1_ffn_expert_b1"].T
        e1[rows, 2463:2469] = a["L1_ffn_expert_b2"].T
        e1[E1N * q:E1N * (q + 1), 2469 + 64 * q:2533 + 64 * q] = a["L1_ffn_expert_b3"]
        for part in (0, 64, 96):
            for e in range(E1N):
                sel2[part + E1N * q + e, e, rows] = 1
    e1[:, 0:2304] = wb.reshape(128, 2304)
    e1[:, 2597:3365] = sel2.reshape(128, 768)
    e1[:, 2444:2450] = a["L1_ffn_router_b2"]
    e1[:, 2450:2456] = np.arange(E1N, 0, -1)
    d["e1"] = e1
    att = np.zeros((128, 138), f4)
    att[0:64, 0:48] = a["L1_attn_C"]
    att[0:48, 48:112] = a["L1_attn_C"].T
    att[0:48, 112:120] = a["L1_attn_M"][:, :, 0]
    att[:, 120:136] = np.kron(np.eye(16), np.ones((CL, 1)))
    att[:, 136], att[:, 137] = dup(a["L1_attn_A"]), dup(a["L1_attn_Bv"])
    d["att"] = att
    d["mphi"] = np.concatenate([a["L1_attn_M_phi_plus"], a["L1_attn_M_phi_minus"]]).reshape(
        2 * KF, F * F)
    return {k: np.ascontiguousarray(v, dtype=f4) for k, v in d.items()}


def kernel(**inputs):
    import concourse.bacc as _bacc
    from concourse import mybir as _mybir
    from concourse.bass_utils import run_bass_kernel_spmd as _run

    nc = _bacc.Bacc("TRN2", target_bir_lowering=False, num_devices=1)
    arrays = _layout(inputs)
    t = {k: nc.dram_tensor("in_" + k, v.shape, _mybir.dt.float32, kind="ExternalInput").ap()
         for k, v in arrays.items()}
    t["out"] = nc.dram_tensor("out_h", (128, PAIRCOLS), _mybir.dt.float32,
                              kind="ExternalOutput").ap()
    fusion_program(nc, t)
    r = _run(nc, [{"in_" + k: v for k, v in arrays.items()}], core_ids=[0])
    out = r.results[0]["out_h"].reshape(2, F, 2, TOK)
    return np.ascontiguousarray(out.transpose(2, 0, 3, 1).reshape(BATCH, TOK, F))
```

```python
import concourse.bass as bass
import concourse.mybir as mybir
import numpy as np
from contextlib import ExitStack

BATCH, CH, TIME, VARS = 4, 64, 128, 64
TXT = 77
PATCH, STRIDE = 16, 8
NPATCH = (TIME + STRIDE - PATCH) // STRIDE + 1
FREQ = PATCH // 2 + 1
F = 64
TOK = VARS * NPATCH + TXT
CHK = 3
TC = TOK // CHK
PAIRCOLS = 2 * TOK
TILES = -(-PAIRCOLS // 128)
PADCOLS = TILES * 128
EPS = 1e-5
D, NS, R, KC = 256, 16, 16, 4
LAYERS = 2
SLOTS = BATCH * CHK
SW = TC + 4
E0, HID0 = 8, 128
SS, KF, KX = 64, 24, 8
CL = 8
NCH = -(-TOK // CL)
AW = CL - 1 + NCH * CL + 1
E1N, RH = 6, 32
XW = (TIME + STRIDE) // 2 * VARS
UW = 2 * TC
BIG = 1e30
LEAD = 3.0 ** (-1 / 3)
SERIES_BELOW = 1.0 / 64
PD = 7
SKIP_AT = 12
POOL_GATE_AT = 3
PE_PIECE_AT = (0, 2, 4)
ACT_PIECE_AT = (1, 2, 4, 6, 4, 7, 5, 7, 8, 9, 10, 11, 12, 13)
DVE_PIECE_AT = (6, 11, 20, 22, 28, 29, 30)
V_PREG, V_PREB, V_POSTG, V_POSTB, V_NFW, V_G0, V_B0 = range(7)
M_CB, M_DTB, M_D, M_NW, M_A = 0, 2, 4, 6, 7
MCOLS = M_A + 2 * NS
W_U, W_G, W_X, W_DT, W_O, W_C = 0, 512, 768, 1024, 1280, 1664
W_SIZE = W_C + MCOLS + 1
V_EPS, V_EPS2, V_LNA, V_CUT = 10, 11, 12, 13
V_SIZE = 14
C_SIZE = 416 + V_SIZE
WPARTS = -(-PADCOLS // 512)
E0_SIZE, E1_SIZE, ATT_SIZE = 2728, 3365, 400


def fusion_program(nc, t):
    fp32, bf16 = mybir.dt.float32, mybir.dt.bfloat16
    ALU, ACT, AX = mybir.AluOpType, mybir.ActivationFunctionType, mybir.AxisListType
    ds = bass.ds
    ctx = ExitStack()
    with ctx:
        def sb(name, shape, dt=fp32):
            return ctx.enter_context(nc.sbuf_tensor(name, shape, dt))

        def sem(name):
            return ctx.enter_context(nc.semaphore(name))

        H = sb("H", [128, PAIRCOLS])
        Z = sb("Z", [128, PADCOLS])
        big1 = sb("big1", [128, (2 * SLOTS + 1) * UW])
        X = big1[:, 0:BATCH * XW].rearrange("p (b m) -> p b m", b=BATCH)
        U = big1[:, 0:(SLOTS + 1) * UW]
        SG = big1[:, (SLOTS + 1) * UW:]
        QB = big1[:, 0:2 * F * SS].rearrange("p (s q e) -> p s q e", s=SS, q=2)
        ZS = big1[:, 2 * F * SS:(2 * F + NCH) * SS].rearrange("p (c s) -> p c s", s=SS)
        big2 = sb("big2", [128, NCH * 128])
        HB = big2[:, 0:2 * NS * TC].rearrange("p (j t) -> p j t", j=2 * NS)
        cut = [2 * NS * TC]

        def scan_buffer(n):
            cut[0] += n
            return big2[:, cut[0] - n:cut[0]]
        dbu = [scan_buffer(UW) for _ in range(2)]
        csb = [scan_buffer(TC) for _ in range(2)]
        prod = [scan_buffer(TC) for _ in range(2)]
        ssmf = scan_buffer(TC)
        bcs = [scan_buffer(184).bitcast(bf16)[:, 0:TC] for _ in range(2)]
        dt_ = [scan_buffer(UW) for _ in range(2)]
        dtu = [scan_buffer(UW), sb("dtu1", [128, UW])[:, :]]
        SH = big2[:, :].rearrange("p (b s c) -> p b s c", b=2, s=SS)
        ZT = big2[:, :].rearrange("p (b g m) -> p b g m", b=2, m=128)
        hn2 = sb("hn2", [128, max(SLOTS * SW, BATCH * AW)])
        LG = hn2[:, 0:AW * BATCH].rearrange("p (q b w) -> p q b w", q=2, b=2)
        nb = sb("nb", [128, 9 * TC])
        sq = [nb[:, i * TC:(i + 1) * TC] for i in range(3)]
        lnv = [nb[:, (3 + i) * TC:(4 + i) * TC] for i in range(3)]
        rstd = [nb[:, (6 + i) * TC:(7 + i) * TC] for i in range(3)]
        sqz = [big2[:, i * TC:(i + 1) * TC] for i in range(3)]
        y1 = nb[:, 0:UW]
        xdt = nb[:, 3 * TC:3 * TC + UW]
        spl = nb[:, 6 * TC:6 * TC + UW]
        res = nb[:, 5 * TC:6 * TC]
        prod += [nb[:, 2 * TC:3 * TC], nb[:, 8 * TC:9 * TC]]
        cst = sb("cst", [128, C_SIZE])
        ident, center, mean = (cst[:, 128 * i:128 * i + 128] for i in range(3))
        selc, vec = cst[:, 384:416], cst[:, 416:416 + V_SIZE]
        ringc = sb("ringc", [128, 32])
        diag = sb("diag", [128, 2, 128])
        centerw, meaneps = diag[:, 0, :], diag[:, 1, :]
        sel = sb("sel", [128, 32], bf16)
        mw = [sb(f"mw{l}", [128, W_SIZE]) for l in range(LAYERS)]
        psum = ctx.enter_context(nc.psum_tensor("psum", [128, 4096], fp32))

        e0 = big1[:, 0:E0_SIZE]
        w1z = big1[:, 0:2048].rearrange("p (e q h) -> p e q h", e=E0, q=2)
        w2s = big1[:, 2048:2560].rearrange("p (e f) -> p e f", e=E0)
        wr0, b1c = big1[:, 2560:2576], big1[:, 2576:2584]
        br0 = big1[:, 2584:2592]
        idx0, b2bd = big1[:, 2592:2600], big1[:, 2600:2728]
        hid = [big2[:, 1101 + i * TC:1101 + (i + 1) * TC] for i in range(4)]
        hsc = [big2[:, 2569 + i * TC:2569 + (i + 1) * TC] for i in range(4)]
        wtok = big2[:, 4096:4096 + PADCOLS].rearrange("p (g c) -> p g c", g=TILES)
        wtf = big2[:, 6400:6400 + PADCOLS]
        wres = big2[:, 8704:8704 + PADCOLS]
        wtb = big2[:, 11008:11008 + PADCOLS // 2].bitcast(bf16)
        rhid = big2[:, 12160:12160 + PADCOLS]
        rt = big2[:, 14464:14464 + 2600]
        w123 = big1[:, 0:2304].rearrange("p (k e m) -> p k e m", k=3, e=E1N)
        rw1, rw2 = big1[:, 2304:2432], big1[:, 2432:2444]
        br1, idx1 = big1[:, 2444:2450], big1[:, 2450:2456]
        rb1, eb12 = big1[:, 2456:2457], big1[:, 2457:2469]
        b3bd, sel2f = big1[:, 2469:2597], big1[:, 2597:3365]
        sel2 = big1[:, 3365:3749].bitcast(bf16).rearrange("p (e m) -> p e m", e=E1N)
        mphi = big1[0:48, 14254:18350]
        wv = mw[0][:, 0:1024].rearrange("p (c s) -> p c s", c=16)
        attc = mw[0][:, 1024:1024 + ATT_SIZE]
        cs, ct, m2 = attc[0:64, 0:48], attc[0:48, 48:112], attc[0:48, 112:120]
        cmask, acol, bcol = attc[:, 120:136], attc[:, 136:137], attc[:, 137:138]
        pw, ab, abr = attc[:, 138:147], attc[:, 147:155], attc[:, 155:163]
        abrep = attc[0:64, 163:291]
        gk = attc[0:48, 291:307].rearrange("p (q j) -> p q j", q=2)
        gfull = attc[0:48, 307:315]
        a8row, apair = attc[:, 315:379], attc[:, 379:395]
        kf, km, kx = (mw[1][:, 256 * i:256 * i + 256].rearrange("p (m e) -> p m e", m=4)
                      for i in range(3))
        xt = nb[:, 0:2304].rearrange("p (k b q d) -> p k b q d", k=9, b=2, q=2)

        def wu(l):
            return mw[l][:, W_U:W_U + 512].rearrange("p (k d) -> p k d", k=2)

        def wx(l):
            return mw[l][:, W_X:W_X + 256].rearrange("p (k m) -> p k m", k=2)

        def wo(l, half, par):
            at = W_O + 192 * half + 64 * (1 - par)
            return mw[l][:, at:at + 128]

        def bank(i, n=TC):
            return psum[:, 512 * i:512 * i + n]

        def col(l, i):
            return mw[l][:, W_C + i:W_C + i + 1]

        wt18 = big2[0:18, 0:4096].rearrange("p (f c) -> p f c", f=F)
        dftm = big2[0:18, 4096:4096 + PATCH]
        gt = big2[:, 4608:5120].rearrange("p (j f) -> p j f", j=8)
        inp = [big2[:, 5120 + 1024 * l:5632 + 1024 * l] for l in range(LAYERS)]
        cwt = [big2[:, 5632 + 1024 * l:6144 + 1024 * l].rearrange("p (k d) -> p k d", k=2)
               for l in range(LAYERS)]

        block = ctx.enter_context(nc.Block())
        w18_loaded = sem("w18_loaded")
        setup_loaded, xload = sem("setup_loaded"), [sem(f"xload{b}") for b in range(BATCH)]
        zeroed = sem("zeroed")
        patch_w_ready, patch_w_copied = sem("patch_w_ready"), sem("patch_w_copied")
        embedded, h_ready = sem("embedded"), sem("h_ready")
        a_exp, scaled, zsq, shifted, mats_ready, tap_step, sp_exp, sp_ln = (
            sem(n) for n in ("a_exp", "scaled", "zsq", "shifted", "mats_ready", "tap_step",
                             "sp_exp", "sp_ln"))
        sp_abs = sem("sp_abs")
        spare = sem("spare")
        e0_loaded, e1_loaded, att_loaded = sem("e0_loaded"), sem("e1_loaded"), sem("att_loaded")
        logits, wtok_ready, wt_mm, wt_cast = (sem(n) for n in (
            "logits", "wtok_ready", "wt_mm", "wt_cast"))
        wt_split, r_step, r_exp, wtok_zero = (sem(n) for n in (
            "wt_split", "r_step", "r_exp", "wtok_zero"))
        h1_ready, gelu_done, wrep, hs_done, e_out, h_e0 = (sem(n) for n in (
            "h1_ready", "gelu_done", "wrep", "hs_done", "e_out", "h_e0"))
        l1_ready, a1_done, l2_ready, a2_done, wrep1, hs1_done, e1_out, h_e1 = (sem(n) for n in (
            "l1_ready", "a1_done", "l2_ready", "a2_done", "wrep1", "hs1_done", "e1_out", "h_e1"))
        rh_mm, rh_done, lg_zero, lg_ready = (sem(n) for n in (
            "rh_mm", "rh_done", "lg_zero", "lg_ready"))
        g_mm, g_ready, kj_mm, kj_ready, p_mm, wv_ready = (sem(n) for n in (
            "g_mm", "g_ready", "kj_mm", "kj_ready", "p_mm", "wv_ready"))
        qb_zero, q_mm, q_even, q_odd = (sem(n) for n in ("qb_zero", "q_mm", "q_even", "q_odd"))
        a_step, xt_mm, xt_ready, v_mm, v_copied, state_done, taps_mm, z_mm, z_copied = (
            sem(n) for n in ("a_step", "xt_mm", "xt_ready", "v_mm", "v_copied", "state_done",
                             "taps_mm", "z_mm", "z_copied"))
        zt_mm, zt_copied, f_out, h_att = (sem(n) for n in ("zt_mm", "zt_copied", "f_out", "h_att"))
        sel2_ready = sem("sel2_ready")
        T_SMALL = 1500
        centered, squared, var_ready = sem("centered"), sem("squared"), sem("var_ready")
        ln_done, rstd_ready, normed = sem("ln_done"), sem("rstd_ready"), sem("normed")
        dve_step = sem("dve_step")
        proj_ready, silu_done = sem("proj_ready"), sem("silu_done")
        outp_ready, z_updated = sem("outp_ready"), sem("z_updated")
        pre_mm, pre_act, bc_cast, pre_dve = sem("pre_mm"), sem("pre_act"), sem("bc_cast"), sem("pre_dve")
        brep, crep, ccopied = sem("brep"), sem("crep"), sem("ccopied")
        da_ready, dbu_done, scanned = sem("da_ready"), sem("dbu_done"), sem("scanned")
        hc_done, y_acc, y_out, gated = sem("hc_done"), sem("y_acc"), sem("y_out"), sem("gated")
        stored = sem("stored")
        CR_SCAN, CR_DBU, CR_HC, CR_YACC, CR_CC, CR_YOUT = 4, 4, 4, 4, 2, 3
        SETUP = 16 * 5
        t["r_soft"], t["r_top"] = 20 + 3, (14, 20 + 19)


        @block.sync
        def _(sp):
            sp.dma_start(big2[0:18, 0:4096 + PATCH], t["w18"]).then_inc(w18_loaded, 16)
            for b in range(2):
                sp.dma_start(X[:, b, :], t["x"][:, b * XW:(b + 1) * XW]).then_inc(xload[b], 16)
            for dst, src in ((cst[:, :], t["cst"]),
                             (big2[:, 5120:7168], t["inp"]), (mw[0][:, :], t["mw0"]),
                             (mw[1][:, :], t["mw1"])):
                sp.dma_start(dst, src).then_inc(setup_loaded, 16)
            sp.dma_start(H[:, :].rearrange("p (b t) -> p b t", b=2)[:, :, VARS * NPATCH:],
                         t["txt"].rearrange("p (b t) -> p b t", b=2)).then_inc(setup_loaded, 16)
            for b in range(2, BATCH):
                sp.dma_start(X[:, b, :], t["x"][:, b * XW:(b + 1) * XW]).then_inc(xload[b], 16)
            sp.wait_ge(z_updated, 15)
            sp.dma_start(e0, t["e0"]).then_inc(e0_loaded, 16)
            sp.dma_start(mphi, t["mphi"]).then_inc(att_loaded, 16)
            sp.dma_start(attc[:, 0:138], t["att"]).then_inc(att_loaded, 16)
            sp.wait_ge(z_mm, SS)
            sp.dma_start(big1[:, 0:E1_SIZE], t["e1"]).then_inc(e1_loaded, 16)
            sp.wait_ge(h_e1, 8)
            sp.dma_start(t["out"], H[:, :]).then_inc(stored, 16)
            sp.wait_ge(stored, 16)

        def scan_pool(pool, l):
            with pool.Fori(0, 2) as bp:
                for si in range(6):
                    s = 6 * bp + si
                    S = 12 * l + s
                    for j in range(2 * NS):
                        n = j // 2
                        if j % 2 == 0:
                            pool.wait_ge(ccopied, 193 * l + 16 * s + n + 1 + CR_CC)
                        pool.wait_ge(y_acc, 32 * S + j - 3 + CR_YACC)
                        pool.wait_ge(scanned, 32 * S + 2 * l + j + 1 + CR_SCAN)
                        nc.gpsimd.tensor_tensor(prod[j % 4], HB[:, j, :], csb[n % 2],
                                                ALU.mult).then_inc(hc_done, 1)
                        if j == POOL_GATE_AT:
                            pool.wait_ge(y_out, 2 * S + CR_YOUT)
                            g = big1[:, ds((SLOTS + s) * UW, UW)]
                            nc.gpsimd.tensor_tensor(g, g, y1, ALU.mult).then_inc(gated, 1)
            pool.wait_ge(y_out, 24 * (l + 1) + CR_YOUT)
            g = SG[:, 11 * UW:12 * UW]
            nc.gpsimd.tensor_tensor(g, g, y1, ALU.mult).then_inc(gated, 1)

        @block.gpsimd
        def _(pool):
            nc.gpsimd.memset(hn2[:, :], 0.0).then_inc(zeroed, 1)
            nc.gpsimd.memset(Z[:, PAIRCOLS:], 0.0).then_inc(zeroed, 1)
            for l in range(LAYERS):
                scan_pool(pool, l)
            pool.wait_ge(z_updated, 15)
            nc.gpsimd.memset(wtok, 0.0).then_inc(wtok_zero, 1)
            nc.gpsimd.memset(hn2[:, 0:BATCH * AW], 0.0).then_inc(lg_zero, 1)
            pool.wait_ge(h_e0, 8)
            nc.gpsimd.memset(big1[:, 0:2 * F * SS], 0.0).then_inc(qb_zero, 1)
            pool.wait_ge(h_att, 22)
            nc.gpsimd.memset(wtok, 0.0).then_inc(wtok_zero, 1)

        def norm_pe(pe, cn, rn, cmat, src, extra, emat):
            with pe.Fori(0, 2) as bp:
                for c in range(3):
                    pe.wait_ge(normed, 6 * cn + 3 * bp + c + 1)
                    nc.tensor.matmul(bank(c), cmat, src[:, ds(bp * TOK + c * TC, TC)],
                                     start=True, stop=True).then_inc(centered, 1)
                for c in range(3):
                    pe.wait_ge(squared, 6 * rn + 3 * bp + c + 1)
                    last = nc.tensor.matmul(bank(3 + c), mean, sq[c], start=True,
                                            stop=extra is None)
                    if extra is not None:
                        pe.wait_ge(zsq, 3 * bp + c + 1)
                        last = nc.tensor.matmul(bank(3 + c), emat, extra[c], start=False, stop=True)
                    last.then_inc(var_ready, 1)

        def rms_pe(pe, l):
            use = 1 + l
            with pe.Fori(0, 2) as bp:
                g = 6 * use + 3 * bp
                for c in range(3):
                    pe.wait_ge(squared, g + c + 1)
                    nc.tensor.matmul(bank(3 + c), mean, sq[c], start=True,
                                     stop=True).then_inc(var_ready, 1)
                for c in range(3):
                    pe.wait_ge(tap_step, 32 * l + 16 * bp + (4, 10, 16)[c])
                    for par in range(2):
                        slot = 6 * bp + 3 * par + c
                        for w in range(4):
                            i = 8 * c + 4 * par + w
                            pe.wait_ge(silu_done, 48 * l + 24 * bp + i + 1)
                            at = bank((0, 1, 6, 7)[w])
                            half, steps = w % 2, (2 if w < 2 else 1)
                            for k in range(steps):
                                wt = (wu(l)[:, k, 128 * half:128 * half + 128] if w < 2 else
                                      mw[l][:, W_G + 128 * half:W_G + 128 * half + 128])
                                last = nc.tensor.matmul(at, wt,
                                                        hn2[:, ds(slot * SW + 3 - 2 * k, TC)],
                                                        start=(k == 0), stop=(k == steps - 1))
                            last.then_inc(proj_ready, 1)

        def pre_pe(pe, l, slot, piece):
            p = 13 * l + slot
            if piece == 0:
                pe.wait_ge(pre_act, 3 * p + 1)
                for k in range(2):
                    last = nc.tensor.matmul(bank(7), wx(l)[:, k, :],
                                            U[:, ds(slot * UW + k * TC, TC)],
                                            start=(k == 0), stop=(k == 1))
            else:
                pe.wait_ge(pre_act, 3 * p + piece + 1)
                if piece == 1:
                    pe.wait_ge(bc_cast, 3 * p + 1)
                last = nc.tensor.matmul(
                    bank(7), mw[l][:, W_DT + 128 * (piece - 1):W_DT + 128 * piece], ssmf,
                    start=True, stop=True)
            last.then_inc(pre_mm, 1)

        def rep_b(pe, l, s, n, q):
            S = 12 * l + s
            pe.wait_ge(dbu_done, 16 * S + n + CR_DBU)
            if n == 0 or n == NS:
                pe.wait_ge(bc_cast, 3 * (13 * l + s + (n // NS)) + 3)
            q = (q + n // NS) % 2
            nc.tensor.matmul(bank(2), sel[:, n % NS:n % NS + 1].broadcast_to([128, 128]),
                             bcs[q], start=True, stop=True).then_inc(brep, 1)

        def rep_c(pe, l, s, n, q):
            pe.wait_ge(ccopied, 193 * l + 16 * s + n + CR_CC)
            q = (q + n // NS) % 2
            m = NS + n % NS
            nc.tensor.matmul(bank(4), sel[:, m:m + 1].broadcast_to([128, 128]),
                             bcs[q], start=True, stop=True).then_inc(crep, 1)

        def sum_state(pe, l, s, n):
            S = 12 * l + s
            for half in range(2):
                j = 2 * n + half
                pe.wait_ge(hc_done, 32 * S + j + 1 + CR_HC)
                if n == 0:
                    pe.wait_ge(y_out, 2 * S + half - 1 + CR_YOUT)
                nc.tensor.matmul(bank(half), ident, prod[j % 4], start=(n == 0),
                                 stop=(n == NS - 1)).then_inc(y_acc, 1)
                if n == SKIP_AT:
                    nc.tensor.matmul(bank(half), diag[:, half, :],
                                     U[:, ds(s * UW + half * TC, TC)], start=False, stop=False)

        def scan_pe(pe, l):
            pe.wait_ge(silu_done, 48 * (l + 1) + 4)
            for piece in range(3):
                pre_pe(pe, l, 0, piece)
            rep_b(pe, l, 0, 0, 0)
            rep_c(pe, l, 0, 0, 0)
            with pe.Fori(0, 2) as bp:
                for si in range(6):
                    s, q = 6 * bp + si, si % 2
                    for n in range(NS):
                        rep_c(pe, l, s, n + 1, q)
                        if n == 0:
                            rep_b(pe, l, s, 1, q)
                        if n < NS - 1:
                            rep_b(pe, l, s, n + 2, q)
                        if n in PE_PIECE_AT:
                            pre_pe(pe, l, s + 1, PE_PIECE_AT.index(n))
                        if n >= 1:
                            sum_state(pe, l, s, n - 1)
                    sum_state(pe, l, s, NS - 1)

        def out_pe(pe, l):
            pe.wait_ge(gated, 13 * (l + 1) + 1)
            pe.wait_ge(da_ready, 388 * (l + 1))
            with pe.Fori(0, 2) as bp:
                for c in range(3):
                    pe.wait_ge(z_updated, 6 * l + 3 * bp + c - 2 + 3)
                    for i in range(4):
                        par, half = i // 2, i % 2
                        slot = 6 * bp + 3 * par + c
                        last = nc.tensor.matmul(bank(c), wo(l, half, par),
                                                SG[:, ds(slot * UW + half * TC, TC)],
                                                start=(i == 0), stop=(i == 3))
                    last.then_inc(outp_ready, 1)

        def spread_pe(pe, use):
            pe.wait_ge(wtok_ready, use + 1)
            for g in range(TILES):
                last = nc.tensor.matmul(psum[:, 512 + 128 * g:640 + 128 * g], wtok[:, g, :], ident,
                                        start=True, stop=True, skip_group_check=True)
                if g % 4 == 3 or g == TILES - 1:
                    last.then_inc(wt_mm, 1)

        def experts0_pe(pe):
            pe.wait_ge(wt_split, 4)
            pe.wait_ge(wt_cast, WPARTS)
            with pe.Fori(0, 3) as kk:
                for r in range(2):
                    k = 2 * kk + r
                    cols = ds(k * TC, TC)
                    pe.wait_ge(h_e0, k + 1)
                    nc.tensor.matmul(bank(4 + r), b2bd, wtf[:, cols], start=True, stop=False,
                                     skip_group_check=True)

                    def down(u):
                        pe.wait_ge(hs_done, 16 * k + u + 1 + 4)
                        par = u % 2
                        nc.tensor.matmul(psum[64 * par:64 * par + 64,
                                              512 * (4 + r):512 * (4 + r) + TC],
                                         w2s[:, u // 2, :], hsc[u % 4], start=False, stop=u >= 14,
                                         skip_group_check=True).then_inc(e_out, 1)

                    for e in range(E0):
                        for par in range(2):
                            u = 2 * e + par
                            pe.wait_ge(gelu_done, 16 * k + u - 1 + 2)
                            nc.tensor.matmul(bank(u % 2), w1z[:, e, par, :], Z[:, cols], start=True,
                                             stop=True).then_inc(h1_ready, 1)
                            pe.wait_ge(hs_done, 16 * k + u - 1 + 4)
                            i = 8 * par + e
                            nc.tensor.matmul(bank(2 + u % 2),
                                             sel[:, i:i + 1].broadcast_to([128, 128]),
                                             wtb[:, cols], start=True, stop=True).then_inc(wrep, 1)
                        if e >= 1:
                            down(2 * e - 2)
                            down(2 * e - 1)
                    down(14)
                    down(15)

        def experts1_pe(pe):
            pe.wait_ge(wt_split, 4 * WPARTS + 4)
            pe.wait_ge(wt_cast, 2 * WPARTS)
            pe.wait_ge(sel2_ready, 1)
            with pe.Fori(0, 3) as kk:
                for r in range(2):
                    k = 2 * kk + r
                    cols = ds(k * TC, TC)
                    pe.wait_ge(h_e1, k + 1)
                    nc.tensor.matmul(bank(6 + r), b3bd, wtf[:, cols], start=True, stop=False)

                    def second(e):
                        pe.wait_ge(a1_done, 6 * k + e + 1 + 2)
                        pe.wait_ge(a2_done, 6 * k + e - 1 + 2)
                        nc.tensor.matmul(bank(2 + e % 2), w123[:, 1, e, :], hid[e % 2], start=True,
                                         stop=True).then_inc(l2_ready, 1)
                        pe.wait_ge(hs1_done, 6 * k + e - 1 + 2)
                        nc.tensor.matmul(bank(4 + e % 2), sel2[:, e, :], wtb[:, cols], start=True,
                                         stop=True).then_inc(wrep1, 1)

                    def third(e):
                        pe.wait_ge(hs1_done, 6 * k + e + 1 + 2)
                        nc.tensor.matmul(bank(6 + r), w123[:, 2, e, :], hsc[2 + e % 2], start=False,
                                         stop=e == E1N - 1).then_inc(e1_out, 1)

                    for e in range(E1N + 2):
                        if e < E1N:
                            pe.wait_ge(a1_done, 6 * k + e - 1 + 2)
                            nc.tensor.matmul(bank(e % 2), w123[:, 0, e, :], Z[:, cols], start=True,
                                             stop=True).then_inc(l1_ready, 1)
                        if 1 <= e <= E1N:
                            second(e - 1)
                        if e >= 2:
                            third(e - 2)

        def filter_pe(pe):
            pe.wait_ge(att_loaded, 32)
            pe.wait_ge(a_step, 20)
            pe.wait_ge(normed, 27)
            nc.tensor.matmul(psum[0:48, 0:8], cs, ab[0:64], start=True, stop=True).then_inc(g_mm, 1)
            nc.tensor.matmul(psum[:, 512:576], abrep, ident[0:64, 0:64], start=True, stop=True,
                             skip_group_check=True)
            nc.tensor.matmul(psum[:, 576:640], pw[0:64, 8:9].broadcast_to([64, 128]),
                             ident[0:64, 0:64], start=True, stop=True,
                             skip_group_check=True).then_inc(p_mm, 1)
            mv = mphi.rearrange("o (d e) -> o e d", e=F)

            def q_group(g):
                if g >= 4:
                    pe.wait_ge(q_even, g - 3)
                    pe.wait_ge(q_odd, g - 3)
                for e in range(8):
                    at = 512 * (2 + g % 4) + SS * e
                    last = nc.tensor.matmul(psum[0:64, at:at + SS], mv[:, 8 * g + e, :], ct,
                                            start=True, stop=True, skip_group_check=True)
                last.then_inc(q_mm, 1)

            for g in range(4):
                q_group(g)
            pe.wait_ge(g_ready, 1)
            for e in range(F):
                last = nc.tensor.matmul(psum[0:64, 3072 + 16 * e:3088 + 16 * e], mv[:, e, :],
                                        attc[0:48, 291:307], start=True, stop=True,
                                        skip_group_check=True)
            last.then_inc(kj_mm, 1)
            for g in range(4, 8):
                q_group(g)
            pe.wait_ge(wv_ready, 1)
            for k in range(9):
                if k >= 2:
                    pe.wait_ge(xt_ready, k - 1)
                for bp in range(2):
                    at = bp * TOK + 128 * k
                    last = nc.tensor.matmul(psum[:, 512 * (k % 2) + 128 * bp:
                                                 512 * (k % 2) + 128 * bp + 128],
                                            Z[:, at:at + 128], ident, start=True, stop=True,
                                            skip_group_check=True)
                last.then_inc(xt_mm, 1)
            pe.wait_ge(q_even, 8)
            pe.wait_ge(q_odd, 8)
            for g in range(4):
                for k in range(9):
                    v = 9 * g + k
                    if g == 0:
                        pe.wait_ge(xt_ready, k + 1)
                    if v >= 2:
                        pe.wait_ge(v_copied, v - 1)
                    n = min(16, NCH - 1 - 16 * k)
                    nc.tensor.matmul(
                        bank(2 + v % 2, 32 * n), xt[:, k, g // 2, :, :].rearrange(
                            "p q d -> p (q d)"), wv[:, 0:n, 32 * (g % 2):32 * (g % 2) + 32],
                        start=True, stop=True).then_inc(v_mm, 1)

            def mix_states(bp):
                for g in range(SS // 2):
                    i = SS // 2 * bp + g
                    pe.wait_ge(state_done, 2 * i + 2)
                    if i >= 2:
                        pe.wait_ge(z_copied, i - 1)
                    for k in range(2):
                        at = 512 * (6 + i % 2) + NCH * k
                        last = nc.tensor.matmul(
                            psum[:, at:at + NCH], QB[:, 2 * g + k, :, :].rearrange(
                                "p q e -> p (q e)"), SH[:, bp, 2 * g + k, :], start=True,
                            stop=True, skip_group_check=True)
                    last.then_inc(z_mm, 1)

            def transpose_mixed(bp):
                pe.wait_ge(z_copied, SS // 2 * (bp + 1))
                for g in range(18):
                    i = 18 * bp + g
                    if i >= 2:
                        pe.wait_ge(zt_copied, i - 1)
                    for k in range(min(4, NCH // 2 - 4 * g)):
                        c = 2 * (4 * g + k)
                        at = 512 * (i % 2) + 128 * k
                        last = nc.tensor.matmul(
                            psum[:, at:at + 128], ZS[:, c:c + 2, :].rearrange("p c s -> p (c s)"),
                            ident, start=True, stop=True, skip_group_check=True)
                    last.then_inc(zt_mm, 1)

            def token_outputs(bp):
                pe.wait_ge(zt_copied, 18 * (bp + 1))
                for g in range(NCH // 2):
                    at = 512 * (2 + 3 * bp) + 16 * g
                    last = nc.tensor.matmul(psum[:, at:at + 16], ZT[:, bp, g, :], apair,
                                            start=True, stop=True, skip_group_check=True)
                last.then_inc(f_out, 1)

            mix_states(0)
            pe.wait_ge(kj_ready, 2)
            pe.wait_ge(lg_ready, 24)
            for i in range(CL):
                if i >= 2:
                    pe.wait_ge(h_att, 2 * (i - 1))
                for m in range(KX // 2):
                    wk = (kf if 2 * m < i else kx if 2 * m == i else km)[:, m, :]
                    for q in range(2):
                        base = CL - 1 + i - 2 * m
                        at = 512 * (4 + i % 2)
                        last = nc.tensor.matmul(
                            psum[64 * q:64 * q + 64, at:at + 2 * NCH], wk,
                            LG[:, q, :, base:base + CL * (NCH - 1) + 1:CL], start=(m == 0),
                            stop=(m == KX // 2 - 1), skip_group_check=True)
                last.then_inc(taps_mm, 1)
            transpose_mixed(0)
            mix_states(1)
            pe.wait_ge(h_att, 16)
            token_outputs(0)
            transpose_mixed(1)
            token_outputs(1)

        @block.tensor
        def _(pe):
            pe.wait_ge(w18_loaded, 16)
            for f in range(F):
                last = nc.tensor.matmul(psum[0:64, f * PATCH:(f + 1) * PATCH], wt18[:, f, :], dftm,
                                        start=True, stop=True, skip_group_check=True)
            last.then_inc(patch_w_ready, 1)
            pe.wait_ge(patch_w_copied, 2)
            for bp in range(2):
                for par in range(2):
                    pe.wait_ge(xload[2 * bp + par], 16)
                for nh in range(2):
                    for j in range(8):
                        for par in range(2):
                            xv = X[:, 2 * bp + par, :].rearrange("p (n r v) -> p n r v", r=4, v=VARS)
                            n0 = 8 * nh + j // 4
                            last = nc.tensor.matmul(
                                psum[64 * par:64 * par + 64,
                                     512 * (1 + 2 * bp + nh):512 * (2 + 2 * bp + nh)],
                                gt[:, j, :], xv[:, n0:n0 + 8, j % 4, :],
                                start=(j == 0), stop=(j == 7))
                last.then_inc(embedded, 1)
            pe.wait_ge(h_ready, 2)
            norm_pe(pe, 0, 0, center, H, None, None)
            for l in range(LAYERS):
                rms_pe(pe, l)
                scan_pe(pe, l)
                out_pe(pe, l)
            pe.wait_ge(z_updated, 15)
            pe.wait_ge(mats_ready, 1)
            norm_pe(pe, 1, 3, centerw, Z, sqz, meaneps)
            pe.wait_ge(normed, 15)
            norm_pe(pe, 2, 4, center, H, None, None)
            pe.wait_ge(normed, 21)
            pe.wait_ge(e0_loaded, 16)
            for g in range(TILES):
                last = nc.tensor.matmul(psum[:, 16 * g:16 * g + 16], Z[:, 128 * g:128 * g + 128],
                                        wr0, start=True, stop=True, skip_group_check=True)
            last.then_inc(logits, 1)
            spread_pe(pe, 0)
            experts0_pe(pe)
            pe.wait_ge(h_e0, 8)
            norm_pe(pe, 3, 5, center, H, None, None)
            filter_pe(pe)
            pe.wait_ge(h_att, 22)
            norm_pe(pe, 4, 6, center, H, None, None)
            pe.wait_ge(normed, 33)
            pe.wait_ge(e1_loaded, 16)
            for k in range(5):
                n = min(512, PADCOLS - 512 * k)
                if k == 0:
                    pe.wait_ge(var_ready, 42)
                last = nc.tensor.matmul(bank(k, n), rw1, Z[:, 512 * k:512 * k + n], start=True,
                                        stop=True)
                last.then_inc(rh_mm, 1)
            pe.wait_ge(rh_done, 5)
            for g in range(TILES):
                last = nc.tensor.matmul(psum[:, 12 * g:12 * g + 12], rhid[:, 128 * g:128 * g + 128],
                                        rw2, start=True, stop=True, skip_group_check=True)
            last.then_inc(logits, 1)
            spread_pe(pe, 1)
            experts1_pe(pe)

        def root_act(act, g, c, scale, bias):
            act.wait_ge(var_ready, g + c + 1)
            nc.scalar.activation(lnv[c], bank(3 + c), ACT.Ln, bias=col_eps(bias),
                                 scale=scale).then_inc(ln_done, 1)
            act.wait_ge(ln_done, g + c + 1)
            nc.scalar.activation(rstd[c], lnv[c], ACT.Exp, scale=-0.5).then_inc(rstd_ready, 1)

        def col_eps(v):
            return vec[:, V_EPS:V_EPS + 1] if v == EPS else vec[:, V_EPS2:V_EPS2 + 1]

        def norm_act(act, cn, rn, scale, bias):
            with act.Fori(0, 2) as bp:
                for c in range(3):
                    act.wait_ge(centered, 6 * cn + 3 * bp + c + 1)
                    nc.scalar.activation(sq[c], bank(c), ACT.Square).then_inc(squared, 1)
                for c in range(3):
                    root_act(act, 6 * rn + 3 * bp, c, scale, bias)

        def rms_act(act, l):
            use = 1 + l
            with act.Fori(0, 2) as bp:
                g = 6 * use + 3 * bp
                for c in range(3):
                    root_act(act, g, c, 1.0, EPS)
                for c in range(3):
                    for par in range(2):
                        slot = 6 * bp + 3 * par + c
                        for w in range(4):
                            i = 8 * c + 4 * par + w
                            half = w % 2
                            act.wait_ge(proj_ready, 48 * l + 24 * bp + i + 1)
                            dst = (U if w < 2 else SG)[:, ds(slot * UW + half * TC, TC)]
                            if w < 2:
                                nc.scalar.activation(dst, bank((0, 1, 6, 7)[w]), ACT.Silu,
                                                     bias=col(l, M_CB + half)).then_inc(silu_done, 1)
                            else:
                                nc.scalar.activation(dst, bank((0, 1, 6, 7)[w]),
                                                     ACT.Silu).then_inc(silu_done, 1)
                nc.scalar.preload_act_table_set("natural_log_exp_and_others")

        def pre_act_piece(act, l, slot, q, piece):
            p = 13 * l + slot
            half = piece % 2
            cols = slice(half * TC, (half + 1) * TC)
            if piece == 0:
                act.wait_ge(pre_mm, 3 * p + 1)
                nc.scalar.activation(ssmf, bank(7), ACT.Identity).then_inc(pre_act, 1)
            elif piece == 1:
                nc.scalar.activation(bcs[q], bank(7), ACT.Identity).then_inc(bc_cast, 1)
            elif piece < 4:
                act.wait_ge(pre_mm, 3 * p + piece)
                nc.scalar.activation(xdt[:, cols], bank(7), ACT.Identity,
                                     bias=col(l, M_DTB + half)).then_inc(pre_act, 1)
            elif piece < 6:
                rows = (slice(64, 128), slice(96, 128))[half]
                act.wait_ge(pre_dve, PD * p + half + 1)
                nc.scalar.activation(bcs[q][rows], res[rows], ACT.Identity).then_inc(bc_cast, 1)
            elif piece < 8:
                act.wait_ge(pre_act, 3 * p + half + 3)
                nc.scalar.activation(spl[:, cols], xdt[:, cols], ACT.Abs).then_inc(sp_abs, 1)
            elif piece < 10:
                act.wait_ge(sp_abs, 2 * p + half + 1)
                nc.scalar.activation(spl[:, cols], spl[:, cols], ACT.Exp, scale=-1.0,
                                     bias=vec[:, V_LNA:V_LNA + 1]).then_inc(sp_exp, 1)
            elif piece < 12:
                act.wait_ge(sp_exp, 2 * p + half + 1)
                nc.scalar.activation(dtu[q][:, cols], spl[:, cols], ACT.Relu,
                                     bias=vec[:, V_CUT:V_CUT + 1])
            else:
                act.wait_ge(pre_dve, PD * p + 4)
                nc.scalar.activation(spl[:, cols], spl[:, cols], ACT.Ln, bias=1.0,
                                     scale=1.0 / LEAD).then_inc(sp_ln, 1)

        def decay_bank(si, j):
            return bank((3, 5, 6)[(2 * NS * si + j) % 3])

        def decay(act, l, s, si, j, q):
            S = 12 * l + s
            n, half = j // 2, j % 2
            act.wait_ge(scanned, 32 * S + 2 * l + j - 2 + CR_SCAN)
            nc.scalar.activation(decay_bank(si, j), dt_[q][:, half * TC:(half + 1) * TC], ACT.Exp,
                                 scale=col(l, M_A + half * NS + n)).then_inc(da_ready, 1)

        def copy_c(act, l, s, n):
            act.wait_ge(crep, 193 * l + 16 * s + n + 1)
            act.wait_ge(hc_done, 32 * (12 * l + s) + 2 * n - 2 + CR_HC)
            nc.scalar.activation(csb[n % 2], bank(4), ACT.Identity).then_inc(ccopied, 1)

        def scan_act(act, l):
            for piece in range(len(ACT_PIECE_AT)):
                pre_act_piece(act, l, 0, 0, piece)
            act.wait_ge(pre_dve, PD * 13 * l + 6)
            for j in range(4):
                decay(act, l, 0, 0, j, 0)
                if j == 1:
                    copy_c(act, l, 0, 0)
            with act.Fori(0, 2) as bp:
                for si in range(6):
                    s, q = 6 * bp + si, si % 2
                    S = 12 * l + s
                    for n in range(1, NS):
                        if n > 1:
                            decay(act, l, s, si, 2 * n, q)
                        copy_c(act, l, s, n)
                        if n > 1:
                            decay(act, l, s, si, 2 * n + 1, q)
                        for piece, at in enumerate(ACT_PIECE_AT):
                            if at == n:
                                pre_act_piece(act, l, s + 1, 1 - q, piece)
                    act.wait_ge(pre_dve, PD * (13 * l + s + 1) + 6)
                    for j in range(2):
                        decay(act, l, s + 1, si + 1, j, 1 - q)
                    copy_c(act, l, s + 1, 0)
                    for half in range(2):
                        act.wait_ge(y_acc, 32 * S + 31 + half + CR_YACC)
                        act.wait_ge(gated, 13 * l + s + 2)
                        nc.scalar.activation(y1[:, half * TC:(half + 1) * TC], bank(half),
                                             ACT.Identity).then_inc(y_out, 1)
                        decay(act, l, s + 1, si + 1, 2 + half, 1 - q)

        def top2_act(act, use):
            act.wait_ge(r_step, t["r_top"][use])
            d = rt[:, T_SMALL + 36 * 4:T_SMALL + 36 * 5]
            nc.scalar.activation(d, d, ACT.Exp).then_inc(r_exp, 1)

        def spread_act(act, use):
            for k in range(WPARTS):
                cols = slice(512 * k, min(512 * k + 512, PADCOLS))
                act.wait_ge(wt_mm, WPARTS * use + k + 1)
                part = psum[:, 512 + cols.start:512 + cols.stop]
                nc.scalar.activation(wtf[:, cols], part, ACT.Identity)
                nc.scalar.activation(wtb[:, cols], part, ACT.Identity).then_inc(wt_cast, 1)

        def filter_act(act):
            act.wait_ge(qb_zero, 1)

            def q_even_group(g):
                act.wait_ge(q_mm, g + 1)
                nc.scalar.activation(QB[0:64, :, 0, 8 * g:8 * g + 8], psum[
                    0:64, 512 * (2 + g % 4):512 * (3 + g % 4)].rearrange("p (e s) -> p s e", e=8),
                    ACT.Identity).then_inc(q_even, 1)

            for g in range(8):
                q_even_group(g)
            for k in range(9):
                act.wait_ge(xt_mm, k + 1)
                nc.scalar.activation(xt[:, k, :, :, :], psum[:, 512 * (k % 2):512 * (k % 2) + 256]
                                     .rearrange("p (b q d) -> p b q d", b=2, q=2),
                                     ACT.Identity).then_inc(xt_ready, 1)
            for v in range(36):
                g, k = v // 9, v % 9
                n = min(16, NCH - 1 - 16 * k)
                act.wait_ge(v_mm, v + 1)
                nc.scalar.activation(
                    SH[:, g // 2, 32 * (g % 2):32 * (g % 2) + 32, 16 * k + 1:16 * k + 1 + n],
                    bank(2 + v % 2, 32 * n).rearrange("p (c s) -> p s c", s=32),
                    ACT.Identity).then_inc(v_copied, 1)
            for i in range(SS):
                g = i % (SS // 2)
                act.wait_ge(z_mm, i + 1)
                if i == SS // 2:
                    act.wait_ge(zt_mm, 18)
                nc.scalar.activation(
                    ZS[:, :, 2 * g:2 * g + 2], bank(6 + i % 2, 2 * NCH).rearrange(
                        "p (k c) -> p c k", k=2), ACT.Identity).then_inc(z_copied, 1)

        @block.scalar
        def _(act):
            act.wait_ge(setup_loaded, SETUP)
            for l in range(LAYERS):
                a_cols = mw[l][:, W_C + M_A:W_C + MCOLS]
                nc.scalar.activation(a_cols, a_cols, ACT.Exp).then_inc(a_exp, 1)
            for bp in range(2):
                act.wait_ge(embedded, bp + 1)
                for nh in range(2):
                    dst = H[:, bp * TOK:bp * TOK + VARS * NPATCH].rearrange(
                        "p (v n) -> p n v", v=VARS)[:, 8 * nh:8 * nh + 8, :]
                    last = nc.scalar.activation(
                        dst, psum[:, 512 * (1 + 2 * bp + nh):512 * (2 + 2 * bp + nh)].rearrange(
                            "p (n v) -> p n v", v=VARS), ACT.Identity)
                last.then_inc(h_ready, 1)
            nc.scalar.preload_act_table_set("natural_log_exp_and_others")
            norm_act(act, 0, 0, 1.0 + EPS, EPS * EPS)
            for l in range(LAYERS):
                rms_act(act, l)
                scan_act(act, l)
            norm_act(act, 1, 3, 1.0, EPS * EPS)
            norm_act(act, 2, 4, 1.0 + EPS, EPS * EPS)
            top2_act(act, 0)
            spread_act(act, 0)
            with act.Fori(0, 3) as kk:
                for r in range(2):
                    k = 2 * kk + r
                    for u in range(16):
                        act.wait_ge(h1_ready, 16 * k + u + 1)
                        act.wait_ge(hs_done, 16 * k + u - 3 + 4)
                        nc.scalar.activation(hid[u % 4], bank(u % 2), ACT.Gelu,
                                             bias=b1c[:, u // 2:u // 2 + 1]).then_inc(gelu_done, 1)
            nc.scalar.preload_act_table_set("natural_log_exp_and_others")
            norm_act(act, 3, 5, 1.0, EPS)
            filter_act(act)
            norm_act(act, 4, 6, 1.0, EPS)
            for k in range(5):
                n = min(512, PADCOLS - 512 * k)
                act.wait_ge(rh_mm, k + 1)
                nc.scalar.activation(rhid[:, 512 * k:512 * k + n], bank(k, n), ACT.Relu,
                                     bias=rb1).then_inc(rh_done, 1)
            act.wait_ge(r_step, t["r_soft"])
            nc.scalar.activation(rt[:, 0:36 * E1N], rt[:, 0:36 * E1N], ACT.Exp).then_inc(r_exp, 1)
            top2_act(act, 1)
            spread_act(act, 1)
            with act.Fori(0, 3) as kk:
                for r in range(2):
                    k = 2 * kk + r
                    for e in range(E1N + 1):
                        if e < E1N:
                            act.wait_ge(l1_ready, 6 * k + e + 1)
                            act.wait_ge(l2_ready, 6 * k + e - 1 + 2)
                            nc.scalar.activation(hid[e % 2], bank(e % 2), ACT.Relu,
                                                 bias=eb12[:, e:e + 1]).then_inc(a1_done, 1)
                        if e >= 1:
                            f = e - 1
                            act.wait_ge(l2_ready, 6 * k + f + 1 + 2)
                            act.wait_ge(hs1_done, 6 * k + f - 1 + 2)
                            nc.scalar.activation(hid[2 + f % 2], bank(2 + f % 2), ACT.Relu,
                                                 bias=eb12[:, 6 + f:7 + f]).then_inc(a2_done, 1)

        def norm_dve(dve, cn, rn, kind):
            with dve.Fori(0, 2) as bp:
                g = 6 * rn + 3 * bp
                if kind == "final":
                    for c in range(3):
                        z = Z[:, ds(bp * TOK + c * TC, TC)]
                        dve.wait_ge(var_ready, g)
                        nc.vector.tensor_tensor(sqz[c], z, z, ALU.mult).then_inc(zsq, 1)
                for c in range(3):
                    dve.wait_ge(rstd_ready, g + c + 1)
                    cols = ds(bp * TOK + c * TC, TC)
                    if kind in ("plain", "lags"):
                        if kind == "lags":
                            dve.wait_ge(lg_zero, 1)
                            for q in range(2):
                                for tap in range(2):
                                    rows = slice(64 * q, 64 * q + 64)
                                    at = q * 2 * AW + bp * AW + CL - 1 + tap + c * TC
                                    nc.vector.tensor_tensor(
                                        hn2[64 * tap:64 * tap + 64, ds(at, TC)], bank(c)[rows],
                                        rstd[c][rows], ALU.mult).then_inc(lg_ready, 1)
                        nc.vector.tensor_tensor(Z[:, cols], bank(c), rstd[c],
                                                ALU.mult).then_inc(normed, 1)
                        continue
                    nc.vector.tensor_tensor(lnv[c], bank(c), rstd[c], ALU.mult).then_inc(scaled, 1)
                    dve.wait_ge(scaled, 6 * cn + 3 * bp + c + 1)
                    if kind == "gain":
                        nc.vector.tensor_scalar(Z[:, cols], lnv[c], vec[:, V_G0:V_G0 + 1],
                                                vec[:, V_B0:V_B0 + 1], ALU.mult,
                                                ALU.add).then_inc(normed, 1)
                    elif kind == "pre":
                        nc.vector.tensor_scalar(Z[:, cols], lnv[c], vec[:, V_PREG:V_PREG + 1],
                                                vec[:, V_PREB:V_PREB + 1], ALU.mult,
                                                ALU.add).then_inc(normed, 1)
                    elif kind == "final":
                        nc.vector.tensor_scalar(lnv[c], lnv[c], vec[:, V_POSTG:V_POSTG + 1],
                                                vec[:, V_POSTB:V_POSTB + 1], ALU.mult,
                                                ALU.add).then_inc(shifted, 1)
                        dve.wait_ge(shifted, 3 * bp + c + 1)
                        nc.vector.tensor_tensor(H[:, cols], H[:, cols], lnv[c],
                                                ALU.add).then_inc(normed, 1)

        def rms_dve(dve, l, then):
            use = 1 + l
            if l == 0:
                dve.wait_ge(normed, 6 + 3)
                dve.wait_ge(embedded, 2)
                then(nc.vector.memset(U[:, SLOTS * UW:], 0.0))
            else:
                dve.wait_ge(z_updated, 6 * l + 3)
            for half in range(2):
                then(nc.vector.tensor_scalar(diag[:, half, :], ident,
                                             col(l, M_D + half), None, ALU.mult))
            with dve.Fori(0, 2) as bp:
                g = 6 * use + 3 * bp
                for c in range(3):
                    z = Z[:, ds(bp * TOK + c * TC, TC)]
                    dve.wait_ge(var_ready, g)
                    nc.vector.tensor_tensor(sq[c], z, z, ALU.mult).then_inc(squared, 1)
                for c in range(3):
                    dve.wait_ge(rstd_ready, g + c + 1)
                    for par in range(2):
                        slot = 6 * bp + 3 * par + c
                        rows = slice(64 * par, 64 * par + 64)
                        at = 32 * l + 16 * bp + (0, 4, 10)[c] + (2, 3, 3)[c] * par
                        if c > 0:
                            dve.wait_ge(tap_step, at)
                            nc.vector.tensor_copy(
                                hn2[:, ds(slot * SW + 1, 3)],
                                hn2[:, ds((slot - 1) * SW + TC + 1, 3)]).then_inc(tap_step, 1)
                            dve.wait_ge(tap_step, at + 1)
                        for tap in range(2):
                            nc.vector.tensor_tensor(
                                hn2[64 * tap:64 * tap + 64, ds(slot * SW + 3 + tap, TC)],
                                Z[rows, ds(bp * TOK + c * TC, TC)], rstd[c][rows],
                                ALU.mult).then_inc(tap_step, 1)

        def pre_dve_piece(dve, l, slot, q, piece):
            p = 13 * l + slot
            b = bcs[q]
            lo, hi = slice(64, 128), slice(96, 128)
            if piece == 0:
                dve.wait_ge(bc_cast, 3 * p + 1)
                dve.wait_ge(pre_act, 3 * p + 2)
                nc.vector.tensor_tensor(res[lo], ssmf[lo], b[lo], ALU.subtract).then_inc(pre_dve, 1)
            elif piece == 1:
                dve.wait_ge(bc_cast, 3 * p + 2)
                nc.vector.tensor_tensor(res[hi], res[hi], b[hi], ALU.subtract).then_inc(pre_dve, 1)
            elif piece == 2:
                dve.wait_ge(sp_exp, 2 * p + 2)
                nc.vector.scalar_tensor_tensor(dt_[q], spl, -0.5 / LEAD ** 2, spl, ALU.add,
                                               ALU.mult).then_inc(pre_dve, 1)
            elif piece == 3:
                dve.wait_ge(pre_dve, PD * p + 3)
                nc.vector.scalar_tensor_tensor(dt_[q], dt_[q], 1.0 / LEAD, spl, ALU.add,
                                               ALU.mult).then_inc(pre_dve, 1)
            elif piece == 4:
                nc.vector.copy_predicated(dt_[q], dtu[q].bitcast(mybir.dt.int32),
                                          spl).then_inc(pre_dve, 1)
            elif piece == 5:
                dve.wait_ge(pre_dve, PD * p + 5)
                nc.vector.scalar_tensor_tensor(dt_[q], xdt, 0.0, dt_[q], ALU.max,
                                               ALU.add).then_inc(pre_dve, 1)
            else:
                dve.wait_ge(pre_dve, PD * p + 6)
                nc.vector.tensor_tensor(dtu[q], dt_[q], U[:, ds(slot * UW, UW)],
                                        ALU.mult).then_inc(pre_dve, 1)

        def drive(dve, l, s, n, q):
            S = 12 * l + s
            dve.wait_ge(brep, 193 * l + 16 * s + n + 1)
            dve.wait_ge(scanned, 32 * S + 2 * l + 2 * n - 2 + CR_SCAN)
            if n == 0:
                dve.wait_ge(pre_dve, PD * (13 * l + s) + 7)
            nc.vector.tensor_tensor(
                dbu[n % 2].rearrange("p (h t) -> p h t", h=2),
                dtu[q].rearrange("p (h t) -> p h t", h=2),
                bank(2).unsqueeze(1).broadcast_to([128, 2, TC]),
                ALU.mult).then_inc(dbu_done, 1)

        def scan_dve(dve, l):
            dve.wait_ge(silu_done, 48 * (l + 1) + 4)
            for piece in range(len(DVE_PIECE_AT)):
                if piece == 4:
                    dve.wait_ge(sp_ln, 2 * (13 * l) + 2)
                    nc.vector.memset(ringc[:, 31:32], 0.0).then_inc(spare, 1)
                pre_dve_piece(dve, l, 0, 0, piece)
            with dve.Fori(0, 2) as bp:
                for si in range(6):
                    s, q, first = 6 * bp + si, si % 2, si % 3 == 0
                    S = 12 * l + s
                    drive(dve, l, s, 0, q)
                    for j in range(2 * NS):
                        if j == DVE_PIECE_AT[4]:
                            dve.wait_ge(sp_ln, 2 * (13 * l + s + 2))
                        n, half = j // 2, j % 2
                        if half == 1 and n + 1 < NS:
                            drive(dve, l, s, n + 1, q)
                        dve.wait_ge(da_ready, 388 * l + 32 * s + j + 1)
                        dve.wait_ge(dbu_done, 16 * S + n + 1 + CR_DBU)
                        nc.vector.tensor_tensor_scan(
                            HB[:, j, :], decay_bank(si, j), dbu[n % 2][:, half * TC:(half + 1) * TC],
                            0.0 if first else HB[:, j, TC - 1:TC], ALU.mult,
                            ALU.add).then_inc(scanned, 1)
                        if j in DVE_PIECE_AT:
                            pre_dve_piece(dve, l, s + 1, 1 - q, DVE_PIECE_AT.index(j))
            dve.wait_ge(da_ready, 388 * l + 386)
            nc.vector.memset(ringc[:, 30:31], 0.0).then_inc(scanned, 2)

        def out_dve(dve, l):
            with dve.Fori(0, 2) as bp:
                for c in range(3):
                    dve.wait_ge(outp_ready, 6 * l + 3 * bp + c + 1)
                    z = Z[:, ds(bp * TOK + c * TC, TC)]
                    nc.vector.tensor_tensor(z, z, bank(c), ALU.add).then_inc(z_updated, 1)

        r_count = [0]

        def route_dve(dve, use, n, br, idx):
            G = 2 * TILES

            def then(ins):
                r_count[0] += 1
                ins.then_inc(r_step, 1)
                dve.wait_ge(r_step, r_count[0])

            def wide(i):
                return rt[:, 288 * i:288 * i + G * n].rearrange("p (g e) -> p g e", e=n)

            def small(i):
                return rt[:, T_SMALL + 36 * i:T_SMALL + 36 * i + 36]

            def spread(v):
                return v.unsqueeze(2).broadcast_to([128, G, n])

            S, eq, oh1, S2, oh2 = (wide(i) for i in range(5))
            row = lambda v: v.unsqueeze(1).broadcast_to([128, G, n])
            then(nc.vector.tensor_tensor(S, psum[:, 0:G * n].rearrange("p (g e) -> p g e", e=n),
                                         row(br), ALU.add))
            if use == 1:
                then(nc.vector.tensor_reduce(small(0), S, AX.X, ALU.max))
                then(nc.vector.tensor_tensor(S, S, spread(small(0)), ALU.subtract))
                assert r_count[0] == t["r_soft"], r_count[0]
                dve.wait_ge(r_exp, 2)
                then(nc.vector.tensor_reduce(small(1), S, AX.X, ALU.add))
                then(nc.vector.reciprocal(small(1), small(1)))
                then(nc.vector.tensor_tensor(S, S, spread(small(1)), ALU.mult))

            def first(src, m, oh):
                then(nc.vector.tensor_reduce(small(m), src, AX.X, ALU.max))
                then(nc.vector.tensor_tensor(eq, src, spread(small(m)), ALU.is_equal))
                then(nc.vector.tensor_tensor(eq, eq, row(idx), ALU.mult))
                then(nc.vector.tensor_reduce(small(3), eq, AX.X, ALU.max))
                then(nc.vector.tensor_tensor(oh, eq, spread(small(3)), ALU.is_equal))

            first(S, 0, oh1)
            then(nc.vector.tensor_scalar(S2, oh1, -BIG, None, ALU.mult))
            then(nc.vector.tensor_tensor(S2, S2, S, ALU.add))
            first(S2, 1, oh2)
            then(nc.vector.tensor_tensor(small(4), small(1), small(0), ALU.subtract))
            assert r_count[0] == t["r_top"][use], r_count[0]
            dve.wait_ge(r_exp, 1 + 2 * use)
            then(nc.vector.tensor_scalar(small(5), small(4), 1.0, None, ALU.add))
            then(nc.vector.reciprocal(small(5), small(5)))
            then(nc.vector.tensor_tensor(small(6), small(4), small(5), ALU.mult))
            then(nc.vector.tensor_tensor(oh1, oh1, spread(small(5)), ALU.mult))
            then(nc.vector.tensor_tensor(oh2, oh2, spread(small(6)), ALU.mult))
            then(nc.vector.tensor_tensor(oh1, oh1, oh2, ALU.add))
            dve.wait_ge(wtok_zero, use + 1)
            for part in (0, 64, 96):
                last = nc.vector.tensor_copy(wtok[:, :, part:part + 2 * n],
                                             oh1.rearrange("p (g q) e -> p g (q e)", q=2))
            last.then_inc(wtok_ready, 1)
            lo, hi = slice(64, 128), slice(96, 128)
            for k in range(WPARTS):
                cols = slice(512 * k, min(512 * k + 512, PADCOLS))
                done = 4 * (WPARTS * use + k)
                dve.wait_ge(wt_cast, WPARTS * use + k + 1)
                nc.vector.tensor_tensor(wres[lo, cols], wtf[lo, cols], wtb[lo, cols],
                                        ALU.subtract).then_inc(wt_split, 1)
                dve.wait_ge(wt_split, done + 1)
                nc.vector.tensor_copy(wtb[lo, cols], wres[lo, cols]).then_inc(wt_split, 1)
                dve.wait_ge(wt_split, done + 2)
                nc.vector.tensor_tensor(wres[hi, cols], wres[hi, cols], wtb[hi, cols],
                                        ALU.subtract).then_inc(wt_split, 1)
                dve.wait_ge(wt_split, done + 3)
                nc.vector.tensor_copy(wtb[hi, cols], wres[hi, cols]).then_inc(wt_split, 1)

        def filter_dve_weights(dve):
            n = [0]

            def then(ins):
                n[0] += 1
                ins.then_inc(a_step, 1)
                dve.wait_ge(a_step, n[0])

            dve.wait_ge(att_loaded, 32)
            nc.vector.memset(pw[:, 0:1], 1.0)
            nc.vector.tensor_copy(pw[:, 1:2], acol)
            nc.vector.tensor_copy(ab[:, 0:1], bcol)
            then(nc.vector.tensor_copy(abr[:, 7:8], bcol))
            for j in range(1, 8):
                then(nc.vector.tensor_tensor(pw[:, j + 1:j + 2], pw[:, j:j + 1], acol, ALU.mult))
            for j in range(1, 8):
                nc.vector.tensor_tensor(abr[:, 7 - j:8 - j], pw[:, j:j + 1], bcol, ALU.mult)
                then(nc.vector.tensor_tensor(ab[:, j:j + 1], pw[:, j:j + 1], bcol, ALU.mult))
            then(nc.vector.tensor_copy(abrep.rearrange("p (c i) -> p c i", c=16),
                                       abr[0:64].unsqueeze(1).broadcast_to([64, 16, 8])))
            then(nc.vector.memset(gfull, 0.0))
            then(nc.vector.memset(apair, 0.0))
            then(nc.vector.tensor_copy(apair[0:64, 0:8], pw[0:64, 1:9]))
            then(nc.vector.tensor_copy(apair[64:128, 8:16], pw[64:128, 1:9]))

        def filter_dve(dve):
            dve.wait_ge(g_mm, 1)
            nc.vector.tensor_tensor(gfull, psum[0:48, 0:8], m2, ALU.add).then_inc(a_step, 1)
            dve.wait_ge(a_step, 21)
            for q in range(2):
                nc.vector.tensor_copy(gk[:, q, 0:4], gfull[:, q:q + 7:2])
                last = nc.vector.tensor_copy(gk[:, q, 4:8], m2[:, q:q + 7:2])
            last.then_inc(g_ready, 1)
            dve.wait_ge(p_mm, 1)
            nc.vector.tensor_copy(a8row, psum[:, 576:640]).then_inc(a_step, 1)
            nc.vector.tensor_tensor(
                wv, psum[:, 512:576].unsqueeze(1).broadcast_to([128, 16, 64]),
                cmask.unsqueeze(2).broadcast_to([128, 16, 64]), ALU.mult).then_inc(wv_ready, 1)
            dve.wait_ge(qb_zero, 1)
            for g in range(8):
                dve.wait_ge(q_even, g + 1)
                nc.vector.tensor_copy(QB[64:128, :, 1, 8 * g:8 * g + 8], psum[
                    0:64, 512 * (2 + g % 4):512 * (3 + g % 4)].rearrange(
                        "p (e s) -> p s e", e=8)).then_inc(q_odd, 1)
                if g == 3:
                    dve.wait_ge(kj_mm, 1)
                    kp = psum[0:64, 3072:4096].rearrange("p (e q f m) -> p q f m e", e=F, q=2, f=2)
                    for q in range(2):
                        rows = slice(64 * q, 64 * q + 64)
                        nc.vector.tensor_copy(kf[rows], kp[:, q, 0, :, :])
                        nc.vector.tensor_copy(km[rows], kp[:, q, 1, :, :])
                        nc.vector.tensor_copy(kx[rows], kp[:, q, q, :, :]).then_inc(kj_ready, 1)
            for bp in range(2):
                nc.vector.memset(SH[:, bp, :, 0:1], 0.0).then_inc(a_step, 1)
            dve.wait_ge(a_step, 24)
            for g in range(4):
                dve.wait_ge(v_copied, 9 * (g + 1))
                for i in range(32):
                    n = 32 * (g % 2) + i
                    line = SH[:, g // 2, n, :]
                    nc.vector.tensor_tensor_scan(
                        line, a8row[:, n:n + 1].broadcast_to([128, NCH]), line, 0.0, ALU.mult,
                        ALU.add).then_inc(state_done, 1)
            for i in range(CL):
                n = NCH if i < TOK - CL * (NCH - 1) else NCH - 1
                dve.wait_ge(taps_mm, i + 1)
                for bp in range(2):
                    at = bp * TOK + i
                    h = H[:, at:at + CL * (n - 1) + 1:CL]
                    nc.vector.tensor_tensor(h, h, psum[:, 512 * (4 + i % 2) + NCH * bp:
                                                       512 * (4 + i % 2) + NCH * bp + n],
                                            ALU.add).then_inc(h_att, 1)
            for bp in range(2):
                for g in range(18):
                    i, n = 18 * bp + g, min(4, NCH // 2 - 4 * g)
                    dve.wait_ge(zt_mm, i + 1)
                    nc.vector.tensor_copy(ZT[:, bp, 4 * g:4 * g + n, :], bank(
                        i % 2, 128 * n).rearrange("p (k m) -> p k m", m=128)).then_inc(zt_copied, 1)
                dve.wait_ge(f_out, bp + 1)
                dve.wait_ge(h_att, 16)
                for c in range(3):
                    n = min(512, TOK - 512 * c)
                    h = H[:, bp * TOK + 512 * c:bp * TOK + 512 * c + n]
                    nc.vector.tensor_tensor(h, h, bank(2 + 3 * bp + c, n),
                                            ALU.add).then_inc(h_att, 1)

        @block.vector
        def _(dve):
            steps = [0]

            def then(ins):
                steps[0] += 1
                ins.then_inc(dve_step, 1)
                dve.wait_ge(dve_step, steps[0])

            for i, (ring, count) in enumerate(((scanned, CR_SCAN), (dbu_done, CR_DBU),
                                               (hc_done, CR_HC), (y_acc, CR_YACC),
                                               (ccopied, CR_CC), (y_out, CR_YOUT), (normed, 3),
                                               (silu_done, 4), (z_updated, 3), (pre_act, 1),
                                               (gated, 1), (gelu_done, 2), (hs_done, 4),
                                               (e_out, 4), (h_e0, 2), (a1_done, 2), (a2_done, 2),
                                               (l2_ready, 2), (hs1_done, 2), (e1_out, 2),
                                               (h_e1, 2))):
                nc.vector.memset(ringc[:, i:i + 1], 0.0).then_inc(ring, count)
            dve.wait_ge(patch_w_ready, 1)
            for par in range(2):
                nc.vector.tensor_copy(
                    gt[64 * par:64 * par + 64], psum[0:64, 0:1024].rearrange(
                        "p (f r j) -> p r j f", r=2, j=8)[:, par]).then_inc(patch_w_copied, 1)
            dve.wait_ge(setup_loaded, SETUP)
            dve.wait_ge(zeroed, 2)
            then(nc.vector.tensor_copy(sel[:, :], selc))
            for l in range(LAYERS):
                for k in range(2):
                    then(nc.vector.tensor_tensor(wu(l)[:, k, :], inp[l][:, 0:D], cwt[l][:, k, :],
                                                 ALU.mult))
                then(nc.vector.tensor_scalar(mw[l][:, W_U:W_U + 512], mw[l][:, W_U:W_U + 512],
                                             col(l, M_NW), None, ALU.mult))
                then(nc.vector.tensor_scalar(mw[l][0:64, W_G:W_G + D], inp[l][0:64, D:2 * D],
                                             col(l, M_NW)[0:64], None, ALU.mult))
            for l in range(LAYERS):
                dve.wait_ge(a_exp, l + 1)
                then(nc.vector.tensor_scalar(mw[l][:, W_C + M_A:W_C + MCOLS],
                                             mw[l][:, W_C + M_A:W_C + MCOLS], -1.0, None, ALU.mult))
            norm_dve(dve, 0, 0, "pre")
            for l in range(LAYERS):
                rms_dve(dve, l, then)
                scan_dve(dve, l)
                out_dve(dve, l)
            then(nc.vector.tensor_scalar(centerw, center, vec[:, V_NFW:V_NFW + 1], None,
                                         ALU.mult))
            nc.vector.tensor_scalar(meaneps, mean, EPS, None, ALU.mult).then_inc(mats_ready, 1)
            norm_dve(dve, 1, 3, "final")
            norm_dve(dve, 2, 4, "gain")
            dve.wait_ge(e0_loaded, 16)
            dve.wait_ge(logits, 1)
            route_dve(dve, 0, E0, br0, idx0)
            with dve.Fori(0, 3) as kk:
                for r in range(2):
                    k = 2 * kk + r
                    for u in range(16):
                        dve.wait_ge(gelu_done, 16 * k + u + 1 + 2)
                        dve.wait_ge(wrep, 16 * k + u + 1)
                        dve.wait_ge(e_out, 16 * k + u - 3 + 4)
                        nc.vector.tensor_tensor(hsc[u % 4], hid[u % 4], bank(2 + u % 2),
                                                ALU.mult).then_inc(hs_done, 1)
                    dve.wait_ge(e_out, 16 * k + 16 + 4)
                    h = H[:, ds(k * TC, TC)]
                    nc.vector.tensor_tensor(h, h, bank(4 + r), ALU.add).then_inc(h_e0, 1)
            filter_dve_weights(dve)
            norm_dve(dve, 3, 5, "lags")
            filter_dve(dve)
            norm_dve(dve, 4, 6, "plain")
            dve.wait_ge(e1_loaded, 16)
            nc.vector.tensor_copy(sel2, sel2f.rearrange("p (e m) -> p e m", e=E1N)).then_inc(
                sel2_ready, 1)
            dve.wait_ge(logits, 2)
            route_dve(dve, 1, E1N, br1, idx1)
            with dve.Fori(0, 3) as kk:
                for r in range(2):
                    k = 2 * kk + r
                    for e in range(E1N):
                        dve.wait_ge(a2_done, 6 * k + e + 1 + 2)
                        dve.wait_ge(wrep1, 6 * k + e + 1)
                        dve.wait_ge(e1_out, 6 * k + e - 1 + 2)
                        nc.vector.tensor_tensor(hsc[2 + e % 2], hid[2 + e % 2], bank(4 + e % 2),
                                                ALU.mult).then_inc(hs1_done, 1)
                    dve.wait_ge(e1_out, 6 * k + 6 + 2)
                    h = H[:, ds(k * TC, TC)]
                    nc.vector.tensor_tensor(h, h, bank(6 + r), ALU.add).then_inc(h_e1, 1)


def _layout(i):
    a = {k: np.asarray(v) for k, v in i.items()}
    f4 = np.float32
    dup = lambda v: np.concatenate([v, v], axis=0)
    d = {}
    x = a["x"].reshape(BATCH, CH, TIME // 2, 2, VARS).transpose(3, 1, 0, 2, 4)
    edge = np.repeat(x[1:2, :, :, -1:, :], STRIDE // 2, axis=3)
    edge = np.concatenate([edge, edge], axis=0)
    d["x"] = np.concatenate([x, edge], axis=3).reshape(128, BATCH * XW)
    w18 = np.zeros((18, 4096 + PATCH), f4)
    w18[:, :4096] = a["L0_tok_W"].reshape(F, 2, FREQ, CH).transpose(1, 2, 0, 3).reshape(18, 4096)
    ang = 2 * np.pi * np.outer(np.arange(FREQ), np.arange(PATCH)) / PATCH
    dft = np.concatenate([np.cos(ang), -np.sin(ang)]) / np.sqrt(PATCH)
    w18[:, 4096:] = dft.reshape(18, 8, 2).transpose(0, 2, 1).reshape(18, PATCH)
    d["w18"] = w18
    cst = np.zeros((128, C_SIZE), f4)
    eye = np.eye(128)
    blk = np.kron(np.eye(2), np.full((F, F), 1.0 / F))
    cst[:, 0:128], cst[:, 128:256], cst[:, 256:384] = eye, eye - blk, blk
    for part in (0, 64, 96):
        cst[part:part + 32, 384:416] = np.eye(32)
    for v, n in ((V_PREG, "L0_attn_pre_g"), (V_PREB, "L0_attn_pre_b"), (V_POSTG, "L0_attn_post_g"),
                 (V_POSTB, "L0_attn_post_b"), (V_NFW, "L0_attn_normf_w"), (V_G0, "L0_ffn_gamma"),
                 (V_B0, "L0_ffn_beta")):
        cst[:, 416 + v] = dup(a[n])
    cst[:, 416 + V_EPS], cst[:, 416 + V_EPS2] = EPS, EPS * EPS
    cst[:, 416 + V_LNA], cst[:, 416 + V_CUT] = np.log(LEAD), -LEAD * SERIES_BELOW
    d["cst"] = cst
    d["txt"] = a["txt"].reshape(2, 2, TXT, F).transpose(1, 3, 0, 2).reshape(128, 2 * TXT)
    inp = np.zeros((128, 2048), f4)
    for l in range(LAYERS):
        inp[:, 1024 * l:1024 * l + 512] = dup(a["L0_attn_inproj_w"][l].T)
        cw = a["L0_attn_conv_w"][l, :, 0, :].T
        for tap in range(2):
            for k in range(2):
                inp[64 * tap:64 * tap + 64, 1024 * l + 512 + 256 * k:1024 * l + 768 + 256 * k] = \
                    cw[KC - 1 - (2 * k + tap)]
        m = np.zeros((128, W_SIZE), f4)
        xp = a["L0_attn_xproj_w"][l].T.reshape(2, 128, R + 2 * NS)
        for h in range(2):
            at = W_X + 128 * h
            for part in (0, 64, 96):
                m[:, at + part:at + part + 32] = xp[h][:, R:]
            m[:, at + 32:at + 48] = xp[h][:, :R]
            m[:, W_O + 192 * h + 64:W_O + 192 * h + 128] = \
                a["L0_attn_outproj_w"][l].T[128 * h:128 * h + 128]
            for c, n in ((M_CB, "conv_b"), (M_DTB, "dtproj_b"), (M_D, "D_param")):
                m[:, W_C + c + h] = a["L0_attn_" + n][l][128 * h:128 * h + 128]
            m[:, W_C + M_A + NS * h:W_C + M_A + NS * (h + 1)] = \
                a["L0_attn_A_log"][l][128 * h:128 * h + 128]
        m[32:48, W_DT:W_DT + D] = a["L0_attn_dtproj_w"][l].T
        m[:, W_C + M_NW] = dup(a["L0_attn_norm_w"][l])
        d[f"mw{l}"] = m
    d["inp"] = inp
    e0 = np.zeros((128, E0_SIZE), f4)
    w1 = e0[:, 0:2048].reshape(128, E0, 2, HID0)
    for q in range(2):
        rows = slice(64 * q, 64 * q + 64)
        w1[rows, :, q, :] = a["L0_ffn_W1"].transpose(1, 0, 2)
        e0[rows, 2560 + 8 * q:2568 + 8 * q] = a["L0_ffn_Wr"]
        e0[8 * q:8 * q + 8, 2600 + 64 * q:2664 + 64 * q] = a["L0_ffn_b2"]
    e0[:, 0:2048] = w1.reshape(128, 2048)
    e0[:, 2048:2560] = a["L0_ffn_W2"].transpose(1, 0, 2).reshape(HID0, E0 * F)
    e0[:, 2576:2584] = a["L0_ffn_b1"].T
    e0[:, 2584:2592] = a["L0_ffn_br"]
    e0[:, 2592:2600] = np.arange(E0, 0, -1)
    d["e0"] = e0
    e1 = np.zeros((128, E1_SIZE), f4)
    wb = np.zeros((128, 3, E1N, 128), f4)
    sel2 = np.zeros((128, E1N, 128), f4)
    for q in range(2):
        rows = slice(64 * q, 64 * q + 64)
        for k in range(3):
            wb[rows, k, :, rows] = a[f"L1_ffn_expert_w{k + 1}"].transpose(1, 0, 2)
        e1[rows, 2304 + RH * q:2304 + RH * (q + 1)] = a["L1_ffn_router_w1"]
        e1[RH * q:RH * (q + 1), 2432 + E1N * q:2432 + E1N * (q + 1)] = a["L1_ffn_router_w2"]
        e1[RH * q:RH * (q + 1), 2456] = a["L1_ffn_router_b1"]
        e1[rows, 2457:2463] = a["L1_ffn_expert_b1"].T
        e1[rows, 2463:2469] = a["L1_ffn_expert_b2"].T
        e1[E1N * q:E1N * (q + 1), 2469 + 64 * q:2533 + 64 * q] = a["L1_ffn_expert_b3"]
        for part in (0, 64, 96):
            for e in range(E1N):
                sel2[part + E1N * q + e, e, rows] = 1
    e1[:, 0:2304] = wb.reshape(128, 2304)
    e1[:, 2597:3365] = sel2.reshape(128, 768)
    e1[:, 2444:2450] = a["L1_ffn_router_b2"]
    e1[:, 2450:2456] = np.arange(E1N, 0, -1)
    d["e1"] = e1
    att = np.zeros((128, 138), f4)
    att[0:64, 0:48] = a["L1_attn_C"]
    att[0:48, 48:112] = a["L1_attn_C"].T
    att[0:48, 112:120] = a["L1_attn_M"][:, :, 0]
    att[:, 120:136] = np.kron(np.eye(16), np.ones((CL, 1)))
    att[:, 136], att[:, 137] = dup(a["L1_attn_A"]), dup(a["L1_attn_Bv"])
    d["att"] = att
    d["mphi"] = np.concatenate([a["L1_attn_M_phi_plus"], a["L1_attn_M_phi_minus"]]).reshape(
        2 * KF, F * F)
    return {k: np.ascontiguousarray(v, dtype=f4) for k, v in d.items()}


def kernel(**inputs):
    import concourse.bacc as _bacc
    from concourse import mybir as _mybir
    from concourse.bass_utils import run_bass_kernel_spmd as _run

    nc = _bacc.Bacc("TRN2", target_bir_lowering=False, num_devices=1)
    arrays = _layout(inputs)
    t = {k: nc.dram_tensor("in_" + k, v.shape, _mybir.dt.float32, kind="ExternalInput").ap()
         for k, v in arrays.items()}
    t["out"] = nc.dram_tensor("out_h", (128, PAIRCOLS), _mybir.dt.float32,
                              kind="ExternalOutput").ap()
    fusion_program(nc, t)
    r = _run(nc, [{"in_" + k: v for k, v in arrays.items()}], core_ids=[0])
    out = r.results[0]["out_h"].reshape(2, F, 2, TOK)
    return np.ascontiguousarray(out.transpose(2, 0, 3, 1).reshape(BATCH, TOK, F))
```
